# Optimizing a Trainium2 kernel written in Bass

```python
import numpy as np
import jax
import jax.numpy as jnp

def _softmax(x, axis=-1):
    return jax.nn.softmax(x, axis=axis)

def _gelu(x):
    return jax.nn.gelu(x, approximate=True)

def _silu(x):
    return jax.nn.silu(x)

def _sigmoid(x):
    return jax.nn.sigmoid(x)

def _layernorm(x, axis=-1, eps=1e-05):
    m = jnp.mean(x, axis=axis, keepdims=True)
    v = jnp.var(x, axis=axis, keepdims=True)
    return (x - m) / jnp.sqrt(v + eps)

def _scatter_add(tgt, idx, src, axis=0):
    return tgt.at[idx].add(src)

def _segment_sum(src, seg, n):
    return jax.ops.segment_sum(src, seg, n)
kernel_name = 'mk_cond_seq_d2_seqx_r4_4c9f06'

def setup_inputs(seed: int=0):
    np.random.seed(seed)
    _w = jnp.asarray

    def _rec_inputs():
        import jax
        import jax.numpy as jnp
        _rk = jax.random.key(seed)
        x = 1.648e-05 + 1 * jax.random.normal(jax.random.fold_in(_rk, 1), (32, 64, 288), jnp.float32)
        _lenS = 64 - jax.random.randint(jax.random.fold_in(_rk, 7), (32,), 0, max(1, 64 // 4) + 1, jnp.int32)
        _lenS2 = 64 - jax.random.randint(jax.random.fold_in(_rk, 8), (32,), 0, max(1, 64 // 4) + 1, jnp.int32)
        cond_1152 = 0.00914911 + 1.00357 * jax.random.normal(jax.random.fold_in(_rk, 11), (32, 288), jnp.float32)
        return (x, cond_1152)
    x, cond_1152 = _rec_inputs()

    def _L0_cond_setup():
        import math
        import jax, jax.numpy as jnp
        import numpy as np
        B, T, D = (8, 256, 288)
        H = 16
        E = 4
        EPS = 1e-06

        def _layer_norm(x):
            mu = jnp.mean(x, axis=-1, keepdims=True)
            var = jnp.mean(jnp.square(x - mu), axis=-1, keepdims=True)
            return (x - mu) * jax.lax.rsqrt(var + EPS)

        def _modulate(x, shift, scale):
            return x * (1.0 + scale) + shift

        def _attention(y, qkv_w, qkv_b, out_w, out_b):
            b, t, d = y.shape
            hd = d // H
            qkv = y @ qkv_w + qkv_b
            q, k, v = jnp.split(qkv, 3, axis=-1)
            q = q.reshape(b, t, H, hd).transpose(0, 2, 1, 3)
            k = k.reshape(b, t, H, hd).transpose(0, 2, 1, 3)
            v = v.reshape(b, t, H, hd).transpose(0, 2, 1, 3)
            scores = jnp.einsum('bhqd,bhkd->bhqk', q, k) / math.sqrt(hd)
            attn = jax.nn.softmax(scores, axis=-1)
            out = jnp.einsum('bhqk,bhkd->bhqd', attn, v)
            out = out.transpose(0, 2, 1, 3).reshape(b, t, d)
            return out @ out_w + out_b
        key = jax.random.key(seed)
        ks = jax.random.split(key, 12)
        std = 0.02
        return {'x': jax.random.normal(ks[0], (B, T, D), dtype=jnp.float32), 'c': jax.random.normal(ks[1], (B, D), dtype=jnp.float32), 'qkv_w': jax.random.normal(ks[2], (D, 3 * D), dtype=jnp.float32) * std, 'qkv_b': jnp.zeros((3 * D,), dtype=jnp.float32), 'out_w': jax.random.normal(ks[3], (D, D), dtype=jnp.float32) * std, 'out_b': jnp.zeros((D,), dtype=jnp.float32), 'w1': jax.random.normal(ks[4], (D, E * D), dtype=jnp.float32) * std, 'b1': jnp.zeros((E * D,), dtype=jnp.float32), 'w2': jax.random.normal(ks[5], (E * D, D), dtype=jnp.float32) * std, 'b2': jnp.zeros((D,), dtype=jnp.float32), 'ada_w': jax.random.normal(ks[6], (D, 6 * D), dtype=jnp.float32) * std, 'ada_b': jnp.zeros((6 * D,), dtype=jnp.float32)}
    _L0_cond_all = _L0_cond_setup()
    _L0_cond_in = {k: v for k, v in _L0_cond_all.items() if k in ('qkv_w', 'qkv_b', 'out_w', 'out_b', 'w1', 'b1', 'w2', 'b2', 'ada_w', 'ada_b')}
    del _L0_cond_all

    def _L1_cond_setup():
        import jax, jax.numpy as jnp
        import numpy as np
        H = 288
        NH = 16
        HD = H // NH
        MLP = int(H * 4.0)
        EPS = 1e-06

        def _ln(z, scale=None):
            m = jnp.mean(z, axis=-1, keepdims=True)
            v = jnp.mean(jnp.square(z - m), axis=-1, keepdims=True)
            y = (z - m) * jax.lax.rsqrt(v + EPS)
            if scale is not None:
                y = y * scale
            return y
        key = jax.random.key(seed)
        ks = jax.random.split(key, 16)
        B, N = (16, 256)
        x = jax.random.normal(ks[0], (B, N, H), dtype=jnp.float32)
        c = jax.random.normal(ks[1], (B, H), dtype=jnp.float32)

        def xav(k, fan_in, fan_out):
            lim = np.sqrt(6.0 / (fan_in + fan_out))
            return jax.random.uniform(k, (fan_in, fan_out), jnp.float32, -lim, lim)
        w_mod = 0.02 * jax.random.normal(ks[2], (H, 6 * H), dtype=jnp.float32)
        b_mod = 0.02 * jax.random.normal(ks[3], (6 * H,), dtype=jnp.float32)
        w_qkv = xav(ks[4], H, 3 * H)
        b_qkv = jnp.zeros((3 * H,), jnp.float32)
        g_q = jnp.ones((HD,), jnp.float32)
        g_k = jnp.ones((HD,), jnp.float32)
        w_proj = xav(ks[5], H, H)
        b_proj = jnp.zeros((H,), jnp.float32)
        w1 = xav(ks[6], H, MLP)
        b1 = jnp.zeros((MLP,), jnp.float32)
        w2 = xav(ks[7], MLP, H)
        b2 = jnp.zeros((H,), jnp.float32)
        return dict(x=x, c=c, w_mod=w_mod, b_mod=b_mod, w_qkv=w_qkv, b_qkv=b_qkv, g_q=g_q, g_k=g_k, w_proj=w_proj, b_proj=b_proj, w1=w1, b1=b1, w2=w2, b2=b2)
    _L1_cond_all = _L1_cond_setup()
    _L1_cond_in = {k: v for k, v in _L1_cond_all.items() if k in ('w_mod', 'b_mod', 'w_qkv', 'b_qkv', 'g_q', 'g_k', 'w_proj', 'b_proj', 'w1', 'b1', 'w2', 'b2')}
    del _L1_cond_all
    return {'x': x, 'cond_1152': cond_1152, 'L0_cond_qkv_w': _L0_cond_in['qkv_w'], 'L0_cond_qkv_b': _L0_cond_in['qkv_b'], 'L0_cond_out_w': _L0_cond_in['out_w'], 'L0_cond_out_b': _L0_cond_in['out_b'], 'L0_cond_w1': _L0_cond_in['w1'], 'L0_cond_b1': _L0_cond_in['b1'], 'L0_cond_w2': _L0_cond_in['w2'], 'L0_cond_b2': _L0_cond_in['b2'], 'L0_cond_ada_w': _L0_cond_in['ada_w'], 'L0_cond_ada_b': _L0_cond_in['ada_b'], 'L1_cond_w_mod': _L1_cond_in['w_mod'], 'L1_cond_b_mod': _L1_cond_in['b_mod'], 'L1_cond_w_qkv': _L1_cond_in['w_qkv'], 'L1_cond_b_qkv': _L1_cond_in['b_qkv'], 'L1_cond_g_q': _L1_cond_in['g_q'], 'L1_cond_g_k': _L1_cond_in['g_k'], 'L1_cond_w_proj': _L1_cond_in['w_proj'], 'L1_cond_b_proj': _L1_cond_in['b_proj'], 'L1_cond_w1': _L1_cond_in['w1'], 'L1_cond_b1': _L1_cond_in['b1'], 'L1_cond_w2': _L1_cond_in['w2'], 'L1_cond_b2': _L1_cond_in['b2']}

def reference(x, cond_1152, L0_cond_qkv_w, L0_cond_qkv_b, L0_cond_out_w, L0_cond_out_b, L0_cond_w1, L0_cond_b1, L0_cond_w2, L0_cond_b2, L0_cond_ada_w, L0_cond_ada_b, L1_cond_w_mod, L1_cond_b_mod, L1_cond_w_qkv, L1_cond_b_qkv, L1_cond_g_q, L1_cond_g_k, L1_cond_w_proj, L1_cond_b_proj, L1_cond_w1, L1_cond_b1, L1_cond_w2, L1_cond_b2):
    import jax
    import jax.numpy as jnp

    def _L0_cond_ref(x, c, qkv_w, qkv_b, out_w, out_b, w1, b1, w2, b2, ada_w, ada_b):
        import math
        import jax, jax.numpy as jnp
        import numpy as np
        B, T, D = (8, 256, 288)
        H = 16
        E = 4
        EPS = 1e-06

        def _layer_norm(x):
            mu = jnp.mean(x, axis=-1, keepdims=True)
            var = jnp.mean(jnp.square(x - mu), axis=-1, keepdims=True)
            return (x - mu) * jax.lax.rsqrt(var + EPS)

        def _modulate(x, shift, scale):
            return x * (1.0 + scale) + shift

        def _attention(y, qkv_w, qkv_b, out_w, out_b):
            b, t, d = y.shape
            hd = d // H
            qkv = y @ qkv_w + qkv_b
            q, k, v = jnp.split(qkv, 3, axis=-1)
            q = q.reshape(b, t, H, hd).transpose(0, 2, 1, 3)
            k = k.reshape(b, t, H, hd).transpose(0, 2, 1, 3)
            v = v.reshape(b, t, H, hd).transpose(0, 2, 1, 3)
            scores = jnp.einsum('bhqd,bhkd->bhqk', q, k) / math.sqrt(hd)
            attn = jax.nn.softmax(scores, axis=-1)
            out = jnp.einsum('bhqk,bhkd->bhqd', attn, v)
            out = out.transpose(0, 2, 1, 3).reshape(b, t, d)
            return out @ out_w + out_b
        mods = (jax.nn.silu(c) @ ada_w + ada_b)[:, None, :]
        m0, m1, m2, m3, m4, m5 = jnp.split(mods, 6, axis=-1)
        y = _modulate(_layer_norm(x), m0, m1)
        x = x + m2 * _attention(y, qkv_w, qkv_b, out_w, out_b)
        y = _modulate(_layer_norm(x), m3, m4)
        y = jax.nn.gelu(y @ w1 + b1, approximate=True)
        x = x + m5 * (y @ w2 + b2)
        return x

    def _L1_cond_ref(x, c, w_mod, b_mod, w_qkv, b_qkv, g_q, g_k, w_proj, b_proj, w1, b1, w2, b2):
        import jax, jax.numpy as jnp
        import numpy as np
        H = 288
        NH = 16
        HD = H // NH
        MLP = int(H * 4.0)
        EPS = 1e-06

        def _ln(z, scale=None):
            m = jnp.mean(z, axis=-1, keepdims=True)
            v = jnp.mean(jnp.square(z - m), axis=-1, keepdims=True)
            y = (z - m) * jax.lax.rsqrt(v + EPS)
            if scale is not None:
                y = y * scale
            return y
        B, N, _ = x.shape
        mod = jax.nn.swish(c) @ w_mod + b_mod
        sh_msa, sc_msa, g_msa, sh_mlp, sc_mlp, g_mlp = jnp.split(mod, 6, axis=1)
        xn = _ln(x) * (1 + sc_msa[:, None, :]) + sh_msa[:, None, :]
        qkv = xn @ w_qkv + b_qkv
        qkv = qkv.reshape(B, N, 3, NH, HD).transpose(2, 0, 3, 1, 4)
        q, k, v = (qkv[0], qkv[1], qkv[2])
        q = _ln(q, g_q)
        k = _ln(k, g_k)
        attn = jax.nn.softmax(jnp.einsum('bhqd,bhkd->bhqk', q, k) * HD ** (-0.5), axis=-1)
        o = jnp.einsum('bhqk,bhkd->bhqd', attn, v)
        o = o.transpose(0, 2, 1, 3).reshape(B, N, H) @ w_proj + b_proj
        x = x + g_msa[:, None, :] * o
        xn2 = _ln(x) * (1 + sc_mlp[:, None, :]) + sh_mlp[:, None, :]
        h = jax.nn.gelu(xn2 @ w1 + b1, approximate=True)
        x = x + g_mlp[:, None, :] * (h @ w2 + b2)
        return x
    x = _L0_cond_ref(x, cond_1152, L0_cond_qkv_w, L0_cond_qkv_b, L0_cond_out_w, L0_cond_out_b, L0_cond_w1, L0_cond_b1, L0_cond_w2, L0_cond_b2, L0_cond_ada_w, L0_cond_ada_b)
    x = _L1_cond_ref(x, cond_1152, L1_cond_w_mod, L1_cond_b_mod, L1_cond_w_qkv, L1_cond_b_qkv, L1_cond_g_q, L1_cond_g_k, L1_cond_w_proj, L1_cond_b_proj, L1_cond_w1, L1_cond_b1, L1_cond_w2, L1_cond_b2)
    return x

_drawn_inputs = setup_inputs


def setup_inputs(seed=0):
    import zlib

    import numpy as np

    out = dict(_drawn_inputs(seed))
    spreads = {'L0_cond_qkv_b': (0.0, 0.8),
     'L0_cond_out_b': (0.0, 0.321),
     'L0_cond_b1': (0.0, 0.8),
     'L0_cond_b2': (0.0, 0.374),
     'L0_cond_ada_b': (0.0, 0.389),
     'L1_cond_b_qkv': (0.0, 0.395),
     'L1_cond_g_q': (1.0, 0.6),
     'L1_cond_g_k': (1.0, 0.6),
     'L1_cond_b_proj': (0.0, 0.405),
     'L1_cond_b1': (0.0, 0.498),
     'L1_cond_b2': (0.0, 0.403)}
    factors = {'L0_cond_qkv_w': 8.0, 'L0_cond_out_w': 5.403, 'L1_cond_b_mod': 5.023}
    for name, (base, spread) in spreads.items():
        noise = np.random.default_rng([zlib.crc32(name.encode()), seed]).standard_normal(out[name].shape)
        drawn = base * np.exp(spread * noise) if base else spread * noise
        out[name] = jnp.asarray(drawn.astype(out[name].dtype))
    for name, factor in factors.items():
        out[name] = (out[name] * factor).astype(out[name].dtype)
    return out
```

```python
from contextlib import ExitStack

import concourse.bass as bass
from concourse import mybir

F32 = mybir.dt.float32
F32R = mybir.dt.float32r
BF16 = mybir.dt.bfloat16
FP16 = mybir.dt.float16
ALU = mybir.AluOpType
ACT = mybir.ActivationFunctionType
AX = mybir.AxisListType

P = 128
B, N, D = 32, 64, 288
H, HD = 16, 18
HP = H // 2
FF = 4 * D
TILES = B * N // P
PAIRS = TILES // 2
EPS = 1e-6
SCALE = float(HD) ** -0.5
A, BB, E, AL, BL = range(5)
E0 = 2 * P
TAIL = D - E0
SLOT = 64
MC = FF // P
SHIFT1, SCALE1, GATE1, SHIFT2, SCALE2, GATE2 = range(6)
PASSES = [(A, A), (A, AL), (AL, A), (BB, BB), (BB, BL), (BL, BB), (E, E)]


class Count:

    def __init__(self, registers, mult=1, add=0):
        self.registers, self.mult, self.add = registers, mult, add

    def __add__(self, n):
        return Count(self.registers, self.mult, self.add + n)

    def __sub__(self, n):
        return self + (-n)

    def __mul__(self, n):
        return Count(self.registers, self.mult * n, self.add * n)

    __radd__, __rmul__ = __add__, __mul__


def at(n):
    return n.registers[n.mult, n.add] if isinstance(n, Count) else n


def counts(engine, s, wanted):
    registers = {(m, a): s * m + a for m, a in wanted}
    for value in registers.values():
        engine.compute_val(value)
    return Count(registers)


def previous(engine, sem, value):
    if isinstance(value, Count) or value > 0:
        engine.wait_ge(sem, at(value))


def settle(engine, sem):
    engine.wait_ge(sem, 1)


def build(nc, io, out):
    ctx = ExitStack()
    with ctx:
        program(nc, ctx, io, out)


def program(nc, ctx, io, out):
    def sb(name, shape, dt=F32):
        return ctx.enter_context(nc.sbuf_tensor(name, shape, dt))

    sems = {}

    def sem(name):
        if name not in sems:
            sems[name] = ctx.enter_context(nc.semaphore(name))
        return sems[name]

    X = sb("X", [P, TILES * D])
    Wqkv = sb("Wqkv", [P, 5, 3 * D], F32R)
    Wout = sb("Wout", [P, 5, D], F32R)
    W1 = sb("W1", [P, 5, FF], F32R)
    W2h = sb("W2h", [P, MC, D], F32R)
    W2l = sb("W2l", [P, MC, D], F32R)
    B2 = sb("B2", [2, D], F32R)
    rawA = sb("rawA", [P, 3, FF])
    rawC = sb("rawC", [P, MC, D])
    raw2 = sb("raw2", [2, D])
    bias = sb("bias", [32, 81])
    biasH = sb("biasH", [32, 81], F32R)
    biasL = sb("biasL", [32, 81])
    mods = [sb(f"mods{l}", [96, 6 * D], BF16) for l in range(2)]
    sel = sb("sel", [96, TILES * P], BF16)
    ident = sb("ident", [P, P])
    ones = sb("ones", [2, P], F32R)
    onesf = sb("onesf", [1, 96])
    cT = sb("cT", [96, 3, 96])
    half = sb("half", [P, 2 * 2 * H])
    gq = sb("gq", [P, HD])
    gk = sb("gk", [P, HD])
    gg = sb("gg", [P, HD])
    ys = [sb(f"ys{j}", [P, 3 * P]) for j in range(2)]
    yT = [sb(f"yT{j}", [P, 5, P], F32R) for j in range(2)]
    st = sb("st", [P, 6])
    mv = sb("mv", [P, 2])
    ve = sb("ve", [P, 1])
    rs = sb("rs", [P, 1])
    qks = sb("qks", [P, 2, H, SLOT], F32R)
    qT = sb("qT", [P, HP, 2, 2, N], F32R)
    kT = sb("kT", [P, HP * P], F32R)
    prob = sb("prob", [P, H * N])
    pTh = sb("pTh", [P, HP, P], FP16)
    pTl = sb("pTl", [P, HP, P], FP16)
    v1 = sb("v1", [P, HP, 2 * HD + 1], BF16)
    v2 = sb("v2", [P, HP, 2 * HD], BF16)
    v3 = sb("v3", [P, HP, 2 * HD], BF16)
    vr = sb("vr", [P, D])
    mx = sb("mx", [P, H])
    rsum = sb("rsum", [P, 2, HP])
    os_ = sb("os", [P, 3 * P])
    oT = sb("oT", [P, 5, P], F32R)
    gate1 = sb("gate1", [P, D])
    gate2 = sb("gate2", [P, 2, D])
    c0, c1 = gate2[0:32, 0, :], gate2[0:32, 1, :]
    tmp = sb("tmp", [P, D])
    tmp2 = sb("tmp2", [P, D])
    y2T = sb("y2T", [P, 5, 2 * P], F32R)
    gl = [sb(f"gl{i}", [P, 2 * P]) for i in range(3)]
    hh = sb("hh", [P, MC, 2 * P], F32R)
    hl = sb("hl", [P, MC, 2 * P], F32R)
    shared = sb("shared", [P, 6 * D])
    adab = shared[0:1, :]
    qk, sq = (shared[:, 2 * a * D:2 * (a + 1) * D].rearrange("p (a h d) -> p a h d", a=2, h=H)
              for a in range(2))
    s1 = sb("s1", [P, 2 * H])
    s2 = sb("s2", [P, 2 * H])
    mu = sb("mu", [P, 2 * H])
    rq = sb("rq", [P, 2 * H])

    bank = [ctx.enter_context(nc.psum_tensor(f"bank{c}", [P, 2, 512], F32)) for c in "XYZM"]
    bX, bY, bZ, bM = bank

    def flat(t):
        return t[:, :, :].rearrange("p a n -> p (a n)")

    t_of = lambda s, j: 2 * s + j
    col = lambda s, l, j: (s * 2 + (j - TILES * l)) * D

    S = {n: sem(n) for n in """
        x_in ada_in raw_qkv_in raw_w1_in raw_w2_in bias_in c_in g_in ada_free bias_lo_in
        zeroed sel_zero sel_made ident_zero ident_made consts pads silu_a silu_b silu_c silu_d c_turned c_copied mods_mm
        mods_a mods_b mods_c mods_d mods_e mods_f bias_h bias_l raw2_h
        wqkv_h wqkv_l w1_h w1_l w2_h w2_l
        bc1 y_turned qkv_mm q_turned k_turned scores p_turned pv_mm o_turned proj_mm bc2 y2_turned bcg out_mm
        gate1_out yTh qk_h v_h q_lay k_lay exps pT_h oT_h y2T_h gate2_out qk_sq
        stats aggr scaled normed spread yTl qk_l v_r v_l q_lay2 maxed shifted pT_l recip onormed ospread oT_l
        gated resid stats2 aggr2 scaled2 normed2 spread2 y2T_l gated2 resid2 qk_sum qk_mean qk_cent qk_var qk_unit
        eps1 rstd1 eps2 rstd2 v_m qk_eps qk_rstd qk_g g_made stored
    """.split()}
    h_mm = [sem(f"h_mm{c}") for c in range(MC)]
    gelu = [sem(f"gelu{c}") for c in range(MC)]
    h_hi = [sem(f"h_hi{c}") for c in range(MC)]
    h_lo = [sem(f"h_lo{c}") for c in range(MC)]

    W = {"qkv": ["L0_cond_qkv_w", "L1_cond_w_qkv"], "out": ["L0_cond_out_w", "L1_cond_w_proj"],
         "w1": ["L0_cond_w1", "L1_cond_w1"], "w2": ["L0_cond_w2", "L1_cond_w2"],
         "ada": ["L0_cond_ada_w", "L1_cond_w_mod"]}
    Bi = {"qkv": ["L0_cond_qkv_b", "L1_cond_b_qkv"], "out": ["L0_cond_out_b", "L1_cond_b_proj"],
          "w1": ["L0_cond_b1", "L1_cond_b1"], "w2": ["L0_cond_b2", "L1_cond_b2"],
          "ada": ["L0_cond_ada_b", "L1_cond_b_mod"]}
    x_rows = io["x"].rearrange("b n d -> (b n) d")
    out_rows = out.rearrange("b n d -> (b n) d")
    LAST = 2 * PAIRS
    BIAS = {"qkv": (0, 27, 0, 3 * D), "out": (27, 36, 3 * D, FF), "w1": (36, 72, 0, FF), "w2": (72, 81, 0, D)}

    block = ctx.enter_context(nc.Block())

    @block.sync
    def _(sp):
        def split_rows(name, l, lo, hi):
            w = io[W[name][l]]
            dmas = [(rawA[:, 0, lo:hi], w[0:P, :]), (rawA[:, 1, lo:hi], w[P:E0, :])]
            return dmas + [(rawA[32 * r:32 * r + 32, 2, lo:hi], w[E0:D, :]) for r in range(3)]

        def load_ada(l):
            w = io[W["ada"][l]].rearrange("(k p) n -> p k n", p=96)
            sp.dma_start(rawA[0:96, :, :], w[:, :, 0:FF]).then_inc(S["ada_in"], 16)
            sp.dma_start(rawC[0:96, 0:6, :].rearrange("p (k a) n -> p k (a n)", k=3),
                         w[:, :, FF:6 * D]).then_inc(S["ada_in"], 16)
            sp.dma_start(adab[:, :], io[Bi["ada"][l]].rearrange("(a n) -> a n", a=1)).then_inc(S["ada_in"], 16)

        def load_qkv_out(l):
            for name in ("qkv", "out"):
                lo, hi = BIAS[name][2:]
                for dst, src in split_rows(name, l, lo, hi):
                    sp.dma_start(dst, src).then_inc(S["raw_qkv_in"], 16)
                sp.dma_start(rawA[96:97, 2, lo:hi], io[Bi[name][l]].rearrange("(a n) -> a n", a=1))\
                    .then_inc(S["raw_qkv_in"], 16)
                sp.dma_start(rawA[97:98, 2, lo:hi], biasL[:, BIAS[name][0]:BIAS[name][1]])\
                    .then_inc(S["raw_qkv_in"], 16)

        def load_w1(l):
            for dst, src in split_rows("w1", l, 0, FF):
                sp.dma_start(dst, src).then_inc(S["raw_w1_in"], 16)
            sp.dma_start(rawA[96:97, 2, :], io[Bi["w1"][l]].rearrange("(a n) -> a n", a=1)).then_inc(S["raw_w1_in"], 16)
            sp.dma_start(rawA[97:98, 2, :], biasL[:, BIAS["w1"][0]:BIAS["w1"][1]]).then_inc(S["raw_w1_in"], 16)

        def load_w2(l):
            sp.dma_start(rawC[:, :, :], io[W["w2"][l]].rearrange("(c p) n -> p c n", p=P)).then_inc(S["raw_w2_in"], 16)
            sp.dma_start(raw2[0:1, :], io[Bi["w2"][l]].rearrange("(a n) -> a n", a=1)).then_inc(S["raw_w2_in"], 16)
            sp.dma_start(raw2[1:2, :], biasL[:, BIAS["w2"][0]:BIAS["w2"][1]]).then_inc(S["raw_w2_in"], 16)

        def load_bias(l):
            for name in ("qkv", "out", "w1", "w2"):
                a, b = BIAS[name][0:2]
                sp.dma_start(bias[:, a:b], io[Bi[name][l]].rearrange("(p n) -> p n", p=32)).then_inc(S["bias_in"], 16)

        sp.dma_start(c0[:, :], io["cond_1152"]).then_inc(S["c_in"], 16)
        load_ada(0)
        load_bias(0)
        for g in range(4):
            sp.dma_start(X[:, g * 4 * D:(g + 1) * 4 * D].rearrange("p (t d) -> p t d", t=4),
                         x_rows[g * 4 * P:(g + 1) * 4 * P, :].rearrange("(t p) d -> p t d", p=P))\
                .then_inc(S["x_in"], 16)
        for dst, name in ((gq, "L1_cond_g_q"), (gk, "L1_cond_g_k")):
            sp.dma_start(dst[:, :], io[name].rearrange("(a n) -> a n", a=1).to_broadcast([P, HD])).then_inc(S["g_in"], 16)
        for l in range(2):
            if l:
                sp.wait_ge(S["w1_h"], 2 * l - 1)
                sp.wait_ge(S["w1_l"], 2 * l - 1)
                sp.wait_ge(S["w2_h"], 2 * l - 1)
                sp.wait_ge(S["w2_l"], 2 * l - 1)
                load_ada(l)
                sp.wait_ge(S["bias_l"], l)
                load_bias(l)
            sp.wait_ge(S["mods_mm"], 2 * l + 2)
            sp.wait_ge(S["bias_l"], l + 1)
            if l == 0:
                sp.wait_ge(S["zeroed"], 1)
            load_qkv_out(l)
            load_w2(l)
            sp.wait_ge(S["wqkv_h"], l + 1)
            sp.wait_ge(S["wqkv_l"], l + 1)
            load_w1(l)

        def store(s):
            for j in range(2):
                sp.wait_ge(S["resid2"], at(t_of(s, j) - 1))
                sp.dma_start(out_rows[bass.ds(at((s * 2 + (j - TILES - 2)) * P), P), :],
                             X[:, bass.ds(at(col(s, 1, j - 2)), D)]).then_inc(S["stored"], 16)

        with sp.Fori(PAIRS + 1, LAST + 1) as s:
            store(counts(sp, s, [(2, -1), (2, 0)] + [(2 * w, (j - TILES - 2) * w) for w in (D, P) for j in range(2)]))
        sp.wait_ge(S["stored"], 16 * TILES)

    @block.gpsimd
    def _(pool):
        pool.memset(rawA[96:128, 2, :], 0.0).then_inc(S["zeroed"], 1)
        pool.wait_ge(S["zeroed"], 1)
        pool.memset(ident[:, :], 0.0).then_inc(S["ident_zero"], 1)
        pool.wait_ge(S["ident_zero"], 1)
        pool.affine_select(out=ident[:, :], in_=ident[:, :], compare_op=ALU.not_equal, fill=1.0, base=0,
                           pattern=[[-1, P]], channel_multiplier=1).then_inc(S["ident_made"], 1)
        pool.wait_ge(S["ident_made"], 1)
        pool.memset(sel[:, :], 0.0).then_inc(S["sel_zero"], 1)
        pool.wait_ge(S["sel_zero"], 1)
        seq = sel[:, :].rearrange("p (m n) -> p m n", n=N)
        for g in range(3):
            pool.affine_select(out=seq, in_=seq, compare_op=ALU.not_equal, fill=1.0, base=-32 * g,
                               pattern=[[-1, B], [0, N]], channel_multiplier=1).then_inc(S["sel_made"], 1)
            pool.wait_ge(S["sel_made"], g + 1)
        pool.wait_ge(S["g_in"], 32)
        pool.tensor_tensor(gg[:, :], gq[:, :], gk[:, :], ALU.mult).then_inc(S["g_made"], 1)

        def row_scale(t, var, eps_sem, out_sem, var_sem):
            settle(pool, S["consts"])
            pool.wait_ge(var_sem, at(t + 1))
            pool.tensor_scalar(ve[:, :], var, EPS, None, ALU.add).then_inc(eps_sem, 1)
            pool.wait_ge(eps_sem, at(t + 1))
            pool.tensor_tensor(rs[:, :], ve[:, :], half[:, 0:1], ALU.pow).then_inc(out_sem, 1)

        def head_scale(t):
            settle(pool, S["consts"])
            pool.wait_ge(S["qk_var"], at(t + 1))
            pool.tensor_scalar(s2[:, :], s2[:, :], 1.0 / HD, EPS, ALU.mult, ALU.add).then_inc(S["qk_eps"], 1)
            pool.wait_ge(S["qk_eps"], at(t + 1))
            pool.tensor_tensor(rq[:, :], s2[:, :], half[:, 0:2 * H], ALU.pow).then_inc(S["qk_rstd"], 1)

        def value_mid(t):
            settle(pool, S["consts"])
            pool.wait_ge(S["v_r"], at(t + 1))
            previous(pool, S["pv_mm"], t)
            pool.tensor_scalar(v2[:, :, :], vr[:, :].rearrange("p (a n) -> p a n", a=HP), 1.0, 0.0,
                               ALU.mult, ALU.add).then_inc(S["v_m"], 1)

        def hidden(s, c):
            settle(pool, S["consts"])
            pool.wait_ge(gelu[c], at(s))
            previous(pool, S["out_mm"], t_of(s, -2))
            pool.tensor_scalar(hh[:, c, :], gl[c % 3][:, :], 1.0, 0.0, ALU.mult, ALU.add).then_inc(h_hi[c], 1)
            pool.wait_ge(h_hi[c], at(s))
            pool.tensor_tensor(hl[:, c, :], gl[c % 3][:, :], hh[:, c, :].bitcast(F32), ALU.subtract)\
                .then_inc(h_lo[c], 1)

        def step(s, attn, mlp):
            chunks = range(MC) if mlp is not None else ()
            at = {0: [0, 1], 1: [2], 2: [3, 4], 3: [5, 6, 7, 8]}
            run = lambda k: [hidden(s, c) for c in chunks if c in at[k]]
            for j in range(2):
                t = t_of(s, j)
                if attn is not None:
                    row_scale(t, mv[:, 1:2], S["eps1"], S["rstd1"], S["aggr"])
                if j == 0:
                    run(0)
                    run(1)
                if attn is not None:
                    value_mid(t)
                    if attn == 1:
                        head_scale(t - TILES)
                if j == 0:
                    run(2)
                    run(3)
                if attn is not None:
                    row_scale(t, mv[:, 1:2], S["eps2"], S["rstd2"], S["aggr2"])

        def wanted(l):
            return [(1, 0), (2, -2), (2, 0), (2, 1), (2, 2)] + [(2, 1 - TILES), (2, 2 - TILES)] * l

        pool.wait_ge(S["consts"], 1)
        step(0, 0, None)
        step(1, 0, 0)
        with pool.Fori(2, PAIRS) as s:
            step(counts(pool, s, wanted(0)), 0, 0)
        step(PAIRS, 1, 0)
        with pool.Fori(PAIRS + 1, LAST) as s:
            step(counts(pool, s, wanted(1)), 1, 1)
        step(LAST, None, 1)

    @block.scalar
    def _(act):
        def cast(dst, src, sem=None):
            i = act.activation(dst, src, ACT.Copy)
            return i.then_inc(sem, 1) if sem is not None else i

        def weights_qkv_out(l):
            act.wait_ge(S["raw_qkv_in"], 16 * 14 * (l + 1))
            previous(act, S["qkv_mm"], TILES * l)
            previous(act, S["proj_mm"], TILES * l)
            for k in range(3):
                cast(Wqkv[:, k, :], rawA[:, k, 0:3 * D])
            cast(Wout[:, 0:3, :], rawA[:, :, 3 * D:FF], S["wqkv_h"])

        def weights_mlp(l):
            act.wait_ge(S["raw_w1_in"], 16 * 7 * (l + 1))
            previous(act, h_mm[MC - 1], PAIRS * l)
            for k in range(3):
                i = cast(W1[:, k, :], rawA[:, k, :])
            i.then_inc(S["w1_h"], 1)
            act.wait_ge(S["raw_w2_in"], 16 * 3 * (l + 1))
            previous(act, S["out_mm"], TILES * l)
            cast(B2[:, :], raw2[:, :])
            cast(W2h[:, :, :], rawC[:, :, :], S["w2_h"])

        def high_bias(l):
            act.wait_ge(S["bias_in"], 64 * (l + 1))
            previous(act, S["bias_l"], l)
            cast(biasH[:, :], bias[:, :], S["bias_h"])

        def gate_one(t):
            act.wait_ge(S["bc1"], at(t + 1))
            previous(act, S["gated"], t)
            cast(gate1[:, :], bZ[:, 0, 0:D], S["gate1_out"])

        def turned_y(t, j):
            act.wait_ge(S["y_turned"], at(t + 1))
            previous(act, S["qkv_mm"], t - 1)
            cast(yT[j][:, 0:3, :], bY[:, 0, 0:3 * P].rearrange("p (k n) -> p k n", k=3), S["yTh"])

        def split_qkv(t, l):
            act.wait_ge(S["qkv_mm"], at(t + 1))
            previous(act, S["k_turned"], t)
            if l == 0:
                q, k = (bZ[:, a, 0:D].rearrange("p (h d) -> p h d", h=H) for a in range(2))
            else:
                act.wait_ge(S["qk_cent"], at(t + 1 - TILES))
                act.activation(sq[:, :, :, :], qk[:, :, :, :], ACT.Square).then_inc(S["qk_sq"], 1)
            previous(act, S["pv_mm"], t)
            cast(v1[:, :, 0:2 * HD], bY[:, 1, 0:D].rearrange("p (a n) -> p a n", a=HP), S["v_h"])
            if l == 1:
                act.wait_ge(S["qk_g"], at(t + 1 - TILES))
                q, k = qk[:, 0, :, :], qk[:, 1, :, :]
            cast(qks[:, 0, :, 0:HD], q)
            cast(qks[:, 0, :, 2 * HD:3 * HD], q)
            cast(qks[:, 1, :, 0:HD], k)
            cast(qks[:, 1, :, HD:2 * HD], k, S["qk_h"])

        def lay_qk(t):
            act.wait_ge(S["q_turned"], at(t + 1))
            previous(act, S["scores"], t)
            cast(qT[0:64, :, :, 0, :], flat(bX)[0:64, :].rearrange("p (a b q) -> p a b q", a=HP, b=2), S["q_lay"])
            act.wait_ge(S["k_turned"], at(t + 1))
            cast(kT[:, :], flat(bY), S["k_lay"])

        def exp(t):
            act.wait_ge(S["shifted"], at(t + 1))
            act.activation(prob[:, :], prob[:, :], ACT.Exp, scale=SCALE).then_inc(S["exps"], 1)

        def turned_p(t):
            act.wait_ge(S["p_turned"], at(t + 1))
            previous(act, S["pv_mm"], t)
            cast(pTh[:, :, :], flat(bX).rearrange("p (a n) -> p a n", a=HP), S["pT_h"])

        def turned_o(t):
            act.wait_ge(S["o_turned"], at(t + 1))
            previous(act, S["proj_mm"], t)
            cast(oT[:, 0:3, :], bZ[:, 0, 0:3 * P].rearrange("p (k n) -> p k n", k=3), S["oT_h"])

        def turned_y2(s, j):
            t = t_of(s, j)
            act.wait_ge(S["y2_turned"], at(t + 1))
            previous(act, h_mm[MC - 1], s)
            cast(y2T[:, 0:3, j * P:(j + 1) * P], bY[:, 0, 0:3 * P].rearrange("p (k n) -> p k n", k=3), S["y2T_h"])

        def gate_two(s):
            act.wait_ge(S["bcg"], at(s))
            previous(act, S["gated2"], t_of(s, -2))
            cast(gate2[:, :, :], bM[:, :, 0:D], S["gate2_out"])

        def hidden(s, c):
            act.wait_ge(h_mm[c], at(s))
            if c >= 3:
                act.wait_ge(h_lo[c - 3], at(s))
            else:
                previous(act, h_lo[MC - 3 + c], s - 1)
            act.activation(gl[c % 3][:, :], bM[:, c % 2, 0:2 * P], ACT.Gelu_apprx_tanh).then_inc(gelu[c], 1)

        def step(s, attn, mlp):
            g = lambda *cs: [hidden(s, c) for c in cs if mlp is not None]
            if mlp is not None:
                gate_two(s)
            if attn is None:
                g(*range(MC))
                return
            for j in range(2):
                t = t_of(s, j)
                h = g if j == 0 else (lambda *cs: None)
                gate_one(t)
                h(0, 1)
                turned_y(t, j)
                h(2)
                split_qkv(t, attn)
                h(3, 4)
                lay_qk(t)
                h(5, 6, 7, 8)
                exp(t)
                turned_p(t)
                turned_o(t)
                turned_y2(s, j)

        def wanted(l):
            return [(1, 0), (1, -1), (2, -2), (2, -1), (2, 0), (2, 1), (2, 2)] + [(2, 1 - TILES), (2, 2 - TILES)] * l

        act.wait_ge(S["c_in"], 16)
        act.activation(c1[:, :], c0[:, :], ACT.Exp, scale=-1.0).then_inc(S["silu_a"], 1)
        high_bias(0)
        weights_qkv_out(0)
        weights_mlp(0)
        step(0, 0, None)
        high_bias(1)
        step(1, 0, 0)
        with act.Fori(2, PAIRS) as s:
            step(counts(act, s, wanted(0)), 0, 0)
        weights_qkv_out(1)
        step(PAIRS, 1, 0)
        weights_mlp(1)
        with act.Fori(PAIRS + 1, LAST) as s:
            step(counts(act, s, wanted(1)), 1, 1)
        step(LAST, None, 1)

    @block.tensor
    def _(pe):
        def product(outs, stationary, moving, sem):
            for n, (a, b) in enumerate(PASSES):
                for o, cols in outs:
                    i = pe.matmul(o, stationary[:, a, :], moving[:, b, cols], start=(n == 0),
                                  stop=(n == len(PASSES) - 1), skip_group_check=True)
            i.then_inc(sem, 1)

        def turn_three(dst, src, sem):
            for k in range(3):
                i = pe.transpose(dst[:, k * P:(k + 1) * P], src[:, k * P:(k + 1) * P], ident[:, :])
            i.then_inc(sem, 1)

        def modulation(l):
            pe.wait_ge(S["ada_in"], 48 * (l + 1))
            for part in range(2):
                if l or part:
                    pe.wait_ge(S["mods_a"], 2 * l + part)
                for m in range(3):
                    b = (bX, bX, bY)[m][0:96, m % 2, 0:D]
                    for k in range(3):
                        c = (3 * part + m) * D
                        w = rawA[0:96, k, c:c + D] if c < FF else \
                            rawC[0:96, 2 * k + (c - FF) // D, :]
                        pe.matmul(b, cT[:, k, :], w, start=(k == 0), stop=False)
                    i = pe.matmul(b, onesf[:, :], adab[:, c:c + D], start=False, stop=True)
                i.then_inc(S["mods_mm"], 1)

        def spread(s, l, j, which, dst):
            tile = bass.ds(at((s * 2 + (j - TILES * l)) * P), P)
            for m, d in zip(which, dst):
                i = pe.matmul(d, sel[:, tile], mods[l][:, m * D:(m + 1) * D], start=True, stop=True)
            return i

        def spread_one(s, l, j):
            t = t_of(s, j)
            previous(pe, S["normed2"], t)
            previous(pe, S["oT_h"], t)
            previous(pe, S["oT_l"], t)
            spread(s, l, j, (SCALE1, SHIFT1, GATE1), (bX[:, 0, 0:D], bX[:, 1, 0:D], bZ[:, 0, 0:D])).then_inc(S["bc1"], 1)

        def turn_y(t, j):
            pe.wait_ge(S["spread"], at(t + 1))
            previous(pe, S["y2T_l"], t)
            previous(pe, S["y2T_h"], t)
            turn_three(bY[:, 0, :], ys[j], S["y_turned"])

        def qkv(t, j):
            pe.wait_ge(S["yTh"], at(t + 1))
            pe.wait_ge(S["yTl"], at(t + 1))
            pe.wait_ge(S["gate1_out"], at(t + 1))
            previous(pe, S["gated"], t)
            product([(bZ[:, 0, 0:D], slice(0, D)), (bZ[:, 1, 0:D], slice(D, 2 * D)), (bY[:, 1, 0:D], slice(2 * D, 3 * D))],
                    yT[j], Wqkv, S["qkv_mm"])

        def turn_qk(t):
            pe.wait_ge(S["qk_h"], at(t + 1))
            pe.wait_ge(S["qk_l"], at(t + 1))
            pe.wait_ge(S["normed"], at(t + 1))
            for which, dst, done in ((0, bX, S["q_turned"]), (1, bY, S["k_turned"])):
                if which:
                    pe.wait_ge(S["v_r"], at(t + 1))
                    pe.wait_ge(S["v_h"], at(t + 1))
                src = qks[:, which, :, :].rearrange("p h c -> p (h c)").bitcast(F32)
                for a in range(HP):
                    i = pe.transpose(flat(dst)[:, a * P:(a + 1) * P], src[:, a * P:(a + 1) * P], ident[:, :])
                i.then_inc(done, 1)

        def scores(t):
            pe.wait_ge(S["q_lay"], at(t + 1))
            pe.wait_ge(S["q_lay2"], at(t + 1))
            pe.wait_ge(S["k_lay"], at(t + 1))
            for a in range(HP):
                for b in range(2):
                    c = (2 * a + b) * N
                    i = pe.matmul(flat(bZ)[:, c:c + N], qT[:, a, b, :, :].rearrange("p h q -> p (h q)"),
                                  kT[:, a * P + b * N:a * P + (b + 1) * N], start=True, stop=True)
            i.then_inc(S["scores"], 1)

        def turn_p(t):
            pe.wait_ge(S["exps"], at(t + 1))
            for a in range(HP):
                i = pe.transpose(flat(bX)[:, a * P:(a + 1) * P], prob[:, a * P:(a + 1) * P], ident[:, :])
            i.then_inc(S["p_turned"], 1)

        def pv(t):
            pe.wait_ge(S["pT_h"], at(t + 1))
            pe.wait_ge(S["pT_l"], at(t + 1))
            pe.wait_ge(S["v_l"], at(t + 1))
            pe.wait_ge(S["v_m"], at(t + 1))
            for a in range(HP):
                for n, (p, v) in enumerate(((pTh, v1), (pTh, v2), (pTh, v3), (pTl, v1), (pTl, v2))):
                    for b in range(2):
                        rows = slice(b * N, (b + 1) * N)
                        w = v.shape[2]
                        c = a * (2 * HD + 1)
                        i = pe.matmul(bY[:, b, c:c + w], p[rows, a, :], v[rows, a, :], start=(n == 0),
                                      stop=(n == 4), skip_group_check=True)
            i.then_inc(S["pv_mm"], 1)

        def turn_o(t):
            pe.wait_ge(S["ospread"], at(t + 1))
            turn_three(bZ[:, 0, :], os_, S["o_turned"])

        def project(t):
            pe.wait_ge(S["oT_h"], at(t + 1))
            pe.wait_ge(S["oT_l"], at(t + 1))
            product([(bZ[:, 1, 0:D], slice(0, D))], oT, Wout, S["proj_mm"])

        def spread_two(s, l, j):
            pe.wait_ge(S["pT_h"], at(t_of(s, j) + 1))
            pe.wait_ge(S["pT_l"], at(t_of(s, j) + 1))
            spread(s, l, j, (SCALE2, SHIFT2), (bX[:, 0, 0:D], bX[:, 1, 0:D])).then_inc(S["bc2"], 1)

        def turn_y2(t, j):
            pe.wait_ge(S["spread2"], at(t + 1))
            pe.wait_ge(S["onormed"], at(t + 1))
            turn_three(bY[:, 0, :], ys[j], S["y2_turned"])

        def spread_gate(s, l):
            previous(pe, S["gated2"], t_of(s, -2))
            for j in range(2):
                i = spread(s, l, j - 2, (GATE2,), (bM[:, j, 0:D],))
            i.then_inc(S["bcg"], 1)

        def hidden(s, c):
            if c == 0:
                pe.wait_ge(S["y2T_h"], at(t_of(s, 0)))
                pe.wait_ge(S["y2T_l"], at(t_of(s, 0)))
            if c < 2:
                pe.wait_ge(S["gate2_out"], at(s))
            else:
                pe.wait_ge(gelu[c - 2], at(s))
            for n, (a, b) in enumerate(PASSES):
                i = pe.matmul(bM[:, c % 2, 0:2 * P], W1[:, a, c * P:(c + 1) * P], y2T[:, b, :],
                              start=(n == 0), stop=(n == len(PASSES) - 1))
            i.then_inc(h_mm[c], 1)

        def second(s, j, chunks):
            o = bM[:, j, 0:D]
            for c in chunks:
                if c == 0:
                    pe.wait_ge(gelu[MC - 1], at(s))
                    if j:
                        pe.wait_ge(gelu[MC - 2], at(s))
                    pe.matmul(o, ones[:, :], B2[:, :], start=True, stop=False)
                if j == 0:
                    pe.wait_ge(h_hi[c], at(s))
                    pe.wait_ge(h_lo[c], at(s))
                tile = slice(j * P, (j + 1) * P)
                for hid, w in ((hh, W2h), (hh, W2l), (hl, W2h)):
                    i = pe.matmul(o, hid[:, c, tile], w[:, c, :], start=False,
                                  stop=(c == MC - 1 and w is W2h and hid is hl))
                if c == MC - 1:
                    i.then_inc(S["out_mm"], 1)

        def step(s, attn, mlp):
            m1 = lambda *cs: [hidden(s, c) for c in cs if mlp is not None]
            m2 = lambda j, *cs: second(s, j, cs) if mlp is not None else None
            if mlp is not None:
                spread_gate(s, mlp)
            if attn is None:
                m1(*range(MC))
                m2(0, *range(MC))
                m2(1, *range(MC))
                return
            spread_one(s, attn, 0)
            m1(0, 1)
            turn_y(t_of(s, 0), 0)
            m1(2)
            qkv(t_of(s, 0), 0)
            m1(3, 4)
            turn_qk(t_of(s, 0))
            m1(5)
            scores(t_of(s, 0))
            m1(6, 7, 8)
            turn_p(t_of(s, 0))
            m2(0, 0, 1, 2)
            pv(t_of(s, 0))
            m2(0, 3, 4)
            turn_o(t_of(s, 0))
            m2(0, 5, 6)
            project(t_of(s, 0))
            spread_two(s, attn, 0)
            m2(0, 7, 8)
            turn_y2(t_of(s, 0), 0)
            spread_one(s, attn, 1)
            turn_y(t_of(s, 1), 1)
            m2(1, 0)
            qkv(t_of(s, 1), 1)
            m2(1, 1, 2)
            turn_qk(t_of(s, 1))
            m2(1, 3)
            scores(t_of(s, 1))
            m2(1, 4, 5, 6)
            turn_p(t_of(s, 1))
            m2(1, 7)
            pv(t_of(s, 1))
            m2(1, 8)
            turn_o(t_of(s, 1))
            project(t_of(s, 1))
            spread_two(s, attn, 1)
            turn_y2(t_of(s, 1), 1)

        def wanted(l):
            tiles = [(2 * P, (j - TILES * l) * P) for j in (-2, -1, 0, 1)]
            return [(1, 0), (2, -2), (2, -1), (2, 0), (2, 1), (2, 2)] + tiles

        pe.wait_ge(S["ident_made"], 1)
        pe.wait_ge(S["silu_d"], 1)
        for k in range(3):
            i = pe.transpose(bZ[0:96, 0, k * 32:(k + 1) * 32], c0[:, k * 96:(k + 1) * 96], ident[0:32, 0:32])
        i.then_inc(S["c_turned"], 1)
        pe.wait_ge(S["c_copied"], 1)
        pe.wait_ge(S["consts"], 1)
        pe.wait_ge(S["sel_made"], 3)
        modulation(0)
        pe.wait_ge(S["mods_f"], 2)
        pe.wait_ge(S["wqkv_h"], 1)
        pe.wait_ge(S["wqkv_l"], 1)
        pe.wait_ge(S["pads"], 1)
        step(0, 0, None)
        pe.wait_ge(S["normed2"], 2)
        pe.wait_ge(S["y2T_h"], 2)
        pe.wait_ge(S["y2T_l"], 2)
        modulation(1)
        pe.wait_ge(S["mods_a"], 4)
        pe.wait_ge(S["w1_h"], 1)
        pe.wait_ge(S["w1_l"], 1)
        pe.wait_ge(S["w2_h"], 1)
        pe.wait_ge(S["w2_l"], 1)
        step(1, 0, 0)
        with pe.Fori(2, PAIRS) as s:
            step(counts(pe, s, wanted(0)), 0, 0)
        pe.wait_ge(S["mods_f"], 4)
        pe.wait_ge(S["wqkv_h"], 2)
        pe.wait_ge(S["wqkv_l"], 2)
        step(PAIRS, 1, 0)
        pe.wait_ge(S["w1_h"], 2)
        pe.wait_ge(S["w1_l"], 2)
        pe.wait_ge(S["w2_h"], 2)
        pe.wait_ge(S["w2_l"], 2)
        with pe.Fori(PAIRS + 1, LAST) as s:
            step(counts(pe, s, wanted(1)), 1, 1)
        step(LAST, None, 1)

    @block.vector
    def _(dve):
        def weights_qkv_out(l):
            dve.wait_ge(S["wqkv_h"], l + 1)
            dve.tensor_tensor(Wqkv[:, AL:BL + 1, :], rawA[:, 0:2, 0:3 * D], Wqkv[:, A:BB + 1, :].bitcast(F32), ALU.subtract)
            dve.tensor_tensor(Wqkv[64:96, E, :], rawA[64:96, 2, 0:3 * D], Wqkv[64:96, E, :].bitcast(F32), ALU.subtract)
            dve.tensor_tensor(Wout[:, AL:BL + 1, :], rawA[:, 0:2, 3 * D:FF], Wout[:, A:BB + 1, :].bitcast(F32), ALU.subtract)
            dve.tensor_tensor(Wout[64:96, E, :], rawA[64:96, 2, 3 * D:FF], Wout[64:96, E, :].bitcast(F32), ALU.subtract)\
                .then_inc(S["wqkv_l"], 1)

        def weights_mlp(l):
            dve.wait_ge(S["w1_h"], l + 1)
            dve.tensor_tensor(W1[:, AL:BL + 1, :], rawA[:, 0:2, :], W1[:, A:BB + 1, :].bitcast(F32), ALU.subtract)
            dve.tensor_tensor(W1[64:96, E, :], rawA[64:96, 2, :], W1[64:96, E, :].bitcast(F32), ALU.subtract)\
                .then_inc(S["w1_l"], 1)
            dve.wait_ge(S["w2_h"], l + 1)
            dve.tensor_tensor(W2l[:, :, :], rawC[:, :, :], W2h[:, :, :].bitcast(F32), ALU.subtract).then_inc(S["w2_l"], 1)

        def modulation(l):
            for part in range(2):
                n = 2 * l + part + 1
                m = mods[l][:, 3 * part * D:3 * (part + 1) * D]
                full = prob[0:96, 0:3 * D]
                dve.wait_ge(S["mods_mm"], n)
                previous(dve, S["mods_f"], n - 1)
                dve.tensor_scalar(prob[0:96, 0:D], bX[0:96, 0, 0:D], 0.0, None, ALU.add)
                dve.tensor_scalar(prob[0:96, D:2 * D], bX[0:96, 1, 0:D], 1.0, None, ALU.add)
                dve.tensor_scalar(prob[0:96, 2 * D:3 * D], bY[0:96, 0, 0:D], 0.0, None, ALU.add).then_inc(S["mods_a"], 1)
                dve.wait_ge(S["mods_a"], n)
                dve.tensor_copy(m, full).then_inc(S["mods_b"], 1)
                dve.wait_ge(S["mods_b"], n)
                for r in (32, 64):
                    i = dve.tensor_tensor(prob[r:r + 32, 0:3 * D], prob[r:r + 32, 0:3 * D], m[r:r + 32, :], ALU.subtract)
                i.then_inc(S["mods_c"], 1)
                dve.wait_ge(S["mods_c"], n)
                for r in (32, 64):
                    i = dve.tensor_copy(m[r:r + 32, :], prob[r:r + 32, 0:3 * D])
                i.then_inc(S["mods_d"], 1)
                dve.wait_ge(S["mods_d"], n)
                dve.tensor_tensor(prob[64:96, 0:3 * D], prob[64:96, 0:3 * D], m[64:96, :], ALU.subtract).then_inc(S["mods_e"], 1)
                dve.wait_ge(S["mods_e"], n)
                dve.tensor_copy(m[64:96, :], prob[64:96, 0:3 * D]).then_inc(S["mods_f"], 1)

        def low_bias(l):
            dve.wait_ge(S["bias_h"], l + 1)
            if l:
                dve.wait_ge(S["w1_h"], 1)
                dve.wait_ge(S["w2_h"], 1)
            dve.tensor_tensor(biasL[:, :], bias[:, :], biasH[:, :].bitcast(F32), ALU.subtract).then_inc(S["bias_l"], 1)

        def norm(s, l, j, sems):
            t = t_of(s, j)
            stats, aggr, rstd, bc, scaled, normed, repeated = sems
            x = X[:, bass.ds(at(col(s, l, j)), D)]
            y = ys[j]
            dve.bn_stats(st[:, :], x).then_inc(stats, 1)
            settle(dve, S["silu_a"])
            dve.wait_ge(stats, at(t + 1))
            dve.bn_aggr(mv[:, :], st[:, :]).then_inc(aggr, 1)
            dve.wait_ge(aggr, at(t + 1))
            dve.wait_ge(bc, at(t + 1))
            dve.scalar_tensor_tensor(y[:, 0:D], x, mv[:, 0:1], bX[:, 0, 0:D], ALU.subtract, ALU.mult).then_inc(scaled, 1)
            dve.wait_ge(scaled, at(t + 1))
            dve.wait_ge(rstd, at(t + 1))
            dve.scalar_tensor_tensor(y[:, 0:D], y[:, 0:D], rs[:, 0:1], bX[:, 1, 0:D], ALU.mult, ALU.add).then_inc(normed, 1)
            dve.wait_ge(normed, at(t + 1))
            dve.tensor_copy(y[:, D:D + 2 * TAIL].rearrange("p (a n) -> p a n", a=2),
                            y[:, E0:D].unsqueeze(1).to_broadcast([P, 2, TAIL])).then_inc(repeated, 1)

        def norm_one(s, l, j):
            t = t_of(s, j)
            settle(dve, S["silu_a"])
            if not isinstance(s, Count):
                dve.wait_ge(S["x_in"], 64)
            previous(dve, S["resid2"], t - TILES + 1 if l else 0)
            previous(dve, S["y2_turned"], t - 1)
            norm(s, l, j, (S["stats"], S["aggr"], S["rstd1"], S["bc1"], S["scaled"], S["normed"], S["spread"]))

        def low(dst, turned, sem, hi_sem, n):
            dve.wait_ge(hi_sem, at(n))
            dve.tensor_tensor(dst[:, AL:BL + 1, :], turned[:, 0:2, :], dst[:, A:BB + 1, :].bitcast(F32), ALU.subtract)
            dve.tensor_tensor(dst[32:64, E, :], turned[32:64, 2, :], dst[32:64, E, :].bitcast(F32), ALU.subtract)\
                .then_inc(sem, 1)

        def turned(bank_):
            return bank_[:, 0, 0:3 * P].rearrange("p (k n) -> p k n", k=3)

        def head_norm(t):
            u = t - TILES
            z = bZ[:, :, 0:D].rearrange("p a (h d) -> p a h d", h=H)
            heads = lambda a: a[:, :].rearrange("p (a h) -> p a h", a=2).unsqueeze(3).to_broadcast([P, 2, H, HD])
            dve.wait_ge(S["qkv_mm"], at(t + 1))
            dve.tensor_reduce(s1[:, :].rearrange("p (a h) -> p a h", a=2), z, AX.X, ALU.add).then_inc(S["qk_sum"], 1)
            dve.wait_ge(S["qk_sum"], at(u + 1))
            dve.tensor_scalar(mu[:, :], s1[:, :], 1.0 / HD, None, ALU.mult).then_inc(S["qk_mean"], 1)
            dve.wait_ge(S["qk_mean"], at(u + 1))
            for read in (S["qk_h"], S["qk_l"]):
                previous(dve, read, t if isinstance(t, Count) or t > TILES else 0)
            for a in range(2):
                i = dve.tensor_tensor(qk[:, a, :, :], z[:, a, :, :], heads(mu)[:, a, :, :], ALU.subtract)
            i.then_inc(S["qk_cent"], 1)
            dve.wait_ge(S["qk_sq"], at(u + 1))
            dve.tensor_reduce(s2[:, :].rearrange("p (a h) -> p a h", a=2), sq[:, :, :, :], AX.X, ALU.add).then_inc(S["qk_var"], 1)

        def head_norm_end(t):
            u = t - TILES
            heads = lambda a: a[:, :].rearrange("p (a h) -> p a h", a=2).unsqueeze(3).to_broadcast([P, 2, H, HD])
            dve.wait_ge(S["qk_rstd"], at(u + 1))
            for a in range(2):
                i = dve.tensor_tensor(qk[:, a, :, :], qk[:, a, :, :], heads(rq)[:, a, :, :], ALU.mult)
            i.then_inc(S["qk_unit"], 1)
            dve.wait_ge(S["qk_unit"], at(u + 1))
            dve.tensor_tensor(qk[:, 0, :, :], qk[:, 0, :, :], gg[:, :].unsqueeze(1).to_broadcast([P, H, HD]), ALU.mult)\
                .then_inc(S["qk_g"], 1)

        def split_qkv(t, l):
            if l:
                head_norm(t)
            dve.wait_ge(S["v_h"], at(t + 1))
            v = bY[:, 1, 0:D].rearrange("p (a n) -> p a n", a=HP)
            r = vr[:, :].rearrange("p (a n) -> p a n", a=HP)
            previous(dve, S["v_l"], t)
            dve.tensor_tensor(r, v, v1[:, :, 0:2 * HD], ALU.subtract).then_inc(S["v_r"], 1)
            if l:
                head_norm_end(t)
            dve.wait_ge(S["qk_h"], at(t + 1))
            if l == 0:
                q, k = (bZ[:, a, 0:D].rearrange("p (h d) -> p h d", h=H) for a in range(2))
            else:
                q, k = qk[:, 0, :, :], qk[:, 1, :, :]
            dve.tensor_tensor(qks[:, 0, :, HD:2 * HD], q, qks[:, 0, :, 0:HD].bitcast(F32), ALU.subtract)
            dve.tensor_tensor(qks[:, 1, :, 2 * HD:3 * HD], k, qks[:, 1, :, 0:HD].bitcast(F32), ALU.subtract).then_inc(S["qk_l"], 1)
            dve.wait_ge(S["v_m"], at(t + 1))
            dve.tensor_tensor(v3[:, :, :], r, v2[:, :, :], ALU.subtract).then_inc(S["v_l"], 1)

        def lay_q(t):
            dve.wait_ge(S["q_turned"], at(t + 1))
            previous(dve, S["scores"], t)
            dve.tensor_copy(qT[64:128, :, :, 1, :], flat(bX)[64:128, :].rearrange("p (a b q) -> p a b q", a=HP, b=2))\
                .then_inc(S["q_lay2"], 1)

        def softmax(t):
            z = flat(bZ).rearrange("p (a n) -> p a n", n=N)
            dve.wait_ge(S["scores"], at(t + 1))
            dve.tensor_reduce(mx[:, :], z, AX.X, ALU.max).then_inc(S["maxed"], 1)
            dve.wait_ge(S["maxed"], at(t + 1))
            previous(dve, S["p_turned"], t)
            dve.tensor_tensor(prob[:, :].rearrange("p (a n) -> p a n", n=N), z,
                              mx[:, :].unsqueeze(2).to_broadcast([P, H, N]), ALU.subtract).then_inc(S["shifted"], 1)

        def low_p(t):
            dve.wait_ge(S["pT_h"], at(t + 1))
            dve.tensor_tensor(pTl[:, :, :], flat(bX).rearrange("p (a n) -> p a n", a=HP), pTh[:, :, :], ALU.subtract)\
                .then_inc(S["pT_l"], 1)

        def normalise(t):
            w = 2 * HD + 1
            dve.wait_ge(S["pv_mm"], at(t + 1))
            acc = bY[:, :, 0:HP * w].rearrange("p b (a n) -> p b a n", n=w)
            dve.reciprocal(rsum[:, :, :], acc[:, :, :, 2 * HD]).then_inc(S["recip"], 1)
            dve.wait_ge(S["recip"], at(t + 1))
            for h in range(2):
                src = slice(h * N, (h + 1) * N)
                for b in range(2):
                    dst = os_[b * N:(b + 1) * N, 0:D].rearrange("p (a h d) -> p a h d", a=HP, h=2)[:, :, h, :]
                    i = dve.tensor_tensor(dst, acc[src, b, :, h * HD:(h + 1) * HD],
                                          rsum[src, b, :].unsqueeze(2).to_broadcast([N, HP, HD]), ALU.mult)
            i.then_inc(S["onormed"], 1)
            dve.wait_ge(S["onormed"], at(t + 1))
            dve.tensor_copy(os_[:, D:D + 2 * TAIL].rearrange("p (a n) -> p a n", a=2),
                            os_[:, E0:D].unsqueeze(1).to_broadcast([P, 2, TAIL])).then_inc(S["ospread"], 1)

        def add_attention(s, l, j):
            t = t_of(s, j)
            x = X[:, bass.ds(at(col(s, l, j)), D)]
            dve.wait_ge(S["proj_mm"], at(t + 1))
            dve.tensor_tensor(tmp[:, :], bZ[:, 1, 0:D], gate1[:, :], ALU.mult).then_inc(S["gated"], 1)
            dve.wait_ge(S["gated"], at(t + 1))
            dve.tensor_tensor(x, x, tmp[:, :], ALU.add).then_inc(S["resid"], 1)

        def add_mlp(s, l, j):
            u = t_of(s, j) - 2
            x = X[:, bass.ds(at(col(s, l, j - 2)), D)]
            dve.wait_ge(S["out_mm"], at(u + 1))
            previous(dve, S["resid2"], u)
            dve.tensor_tensor(tmp2[:, :], bM[:, j, 0:D], gate2[:, j, :], ALU.mult).then_inc(S["gated2"], 1)
            dve.wait_ge(S["gated2"], at(u + 1))
            dve.tensor_tensor(x, x, tmp2[:, :], ALU.add).then_inc(S["resid2"], 1)

        def step(s, attn, mlp):
            for j in range(2):
                if attn is not None:
                    t = t_of(s, j)
                    norm_one(s, attn, j)
                    low(yT[j], turned(bY), S["yTl"], S["yTh"], t + 1)
                    split_qkv(t, attn)
                    lay_q(t)
                    softmax(t)
                    low_p(t)
                    normalise(t)
                    low(oT, turned(bZ), S["oT_l"], S["oT_h"], t + 1)
                    add_attention(s, attn, j)
                    settle(dve, S["silu_a"])
                    dve.wait_ge(S["resid"], at(t + 1))
                    norm(s, attn, j, (S["stats2"], S["aggr2"], S["rstd2"], S["bc2"], S["scaled2"], S["normed2"], S["spread2"]))
                    low(y2T[:, :, j * P:(j + 1) * P], turned(bY), S["y2T_l"], S["y2T_h"], t + 1)
                if mlp is not None:
                    add_mlp(s, mlp, j)

        def wanted(l):
            cols = [(2 * D, (j - TILES * l) * D) for j in (-2, -1, 0, 1)]
            return [(2, -2), (2, -1), (2, 0), (2, 1), (2, 2)] + [(2, n - TILES) for n in (1, 2)] * l + cols

        dve.memset(half[:, :], -0.5)
        dve.memset(onesf[:, :], 1.0)
        dve.memset(ones[:, :].bitcast(F32), 1.0)
        for t_ in (ys[0], ys[1], os_):
            dve.memset(t_[:, D + 2 * TAIL:3 * P], 1.0)
        i = dve.memset(v1[:, :, 2 * HD:2 * HD + 1], 1.0)
        i.then_inc(S["consts"], 1)
        dve.memset(qks[:, :, :, 3 * HD:SLOT].bitcast(F32), 0.0)
        dve.memset(qT[0:64, :, :, 1, :].bitcast(F32), 0.0)
        dve.memset(qT[64:128, :, :, 0, :].bitcast(F32), 0.0).then_inc(S["pads"], 1)
        dve.wait_ge(S["silu_a"], 1)
        dve.tensor_scalar(c1[:, :], c1[:, :], 1.0, None, ALU.add).then_inc(S["silu_b"], 1)
        dve.wait_ge(S["silu_b"], 1)
        dve.reciprocal(c1[:, :], c1[:, :]).then_inc(S["silu_c"], 1)
        dve.wait_ge(S["silu_c"], 1)
        dve.tensor_tensor(c0[:, :], c0[:, :], c1[:, :], ALU.mult).then_inc(S["silu_d"], 1)
        dve.wait_ge(S["c_turned"], 1)
        for k in range(3):
            i = dve.tensor_copy(cT[:, k, :].rearrange("p (r n) -> p r n", r=3),
                                bZ[0:96, 0, k * 32:(k + 1) * 32].unsqueeze(1).to_broadcast([96, 3, 32]))
        i.then_inc(S["c_copied"], 1)
        low_bias(0)
        modulation(0)
        weights_qkv_out(0)
        weights_mlp(0)
        step(0, 0, None)
        dve.wait_ge(S["p_turned"], 2)
        modulation(1)
        low_bias(1)
        step(1, 0, 0)
        with dve.Fori(2, PAIRS) as s:
            step(counts(dve, s, wanted(0)), 0, 0)
        weights_qkv_out(1)
        step(PAIRS, 1, 0)
        weights_mlp(1)
        with dve.Fori(PAIRS + 1, LAST) as s:
            step(counts(dve, s, wanted(1)), 1, 1)
        step(LAST, None, 1)


_OUT = ((B, N, D), "float32")


def kernel(**inputs):
    import numpy as _np
    import concourse.bacc as _bacc
    from concourse import mybir as _mybir
    from concourse.bass_utils import run_bass_kernel_spmd as _run

    nc = _bacc.Bacc("TRN2", target_bir_lowering=False, num_devices=1)
    arrays, io = {}, {}
    for name, value in inputs.items():
        a = _np.ascontiguousarray(value)
        arrays[f"in_{name}_dram"] = a
        io[name] = nc.dram_tensor(f"in_{name}_dram", a.shape, _mybir.dt.from_np(a.dtype), kind="ExternalInput").ap()
    shape, dtype = _OUT
    out = nc.dram_tensor("out_0_dram", shape, _mybir.dt.from_np(_np.dtype(dtype)), kind="ExternalOutput").ap()
    build(nc, io, out)
    r = _run(nc, [arrays], core_ids=[0])
    return r.results[0]["out_0_dram"]
```

```python
from contextlib import ExitStack

import concourse.bass as bass
from concourse import mybir

F32 = mybir.dt.float32
F32R = mybir.dt.float32r
BF16 = mybir.dt.bfloat16
FP16 = mybir.dt.float16
ALU = mybir.AluOpType
ACT = mybir.ActivationFunctionType
AX = mybir.AxisListType

P = 128
B, N, D = 32, 64, 288
H, HD = 16, 18
HP = H // 2
FF = 4 * D
TILES = B * N // P
PAIRS = TILES // 2
EPS = 1e-6
SCALE = float(HD) ** -0.5
A, BB, E, AL, BL = range(5)
E0 = 2 * P
TAIL = D - E0
SLOT = 64
MC = FF // P
SHIFT1, SCALE1, GATE1, SHIFT2, SCALE2, GATE2 = range(6)
PASSES = [(A, A), (A, AL), (AL, A), (BB, BB), (BB, BL), (BL, BB), (E, E)]


class Count:

    def __init__(self, registers, mult=1, add=0):
        self.registers, self.mult, self.add = registers, mult, add

    def __add__(self, n):
        return Count(self.registers, self.mult, self.add + n)

    def __sub__(self, n):
        return self + (-n)

    def __mul__(self, n):
        return Count(self.registers, self.mult * n, self.add * n)

    __radd__, __rmul__ = __add__, __mul__


def at(n):
    return n.registers[n.mult, n.add] if isinstance(n, Count) else n


def counts(engine, s, wanted):
    registers = {(m, a): s * m + a for m, a in wanted}
    for value in registers.values():
        engine.compute_val(value)
    return Count(registers)


def previous(engine, sem, value):
    if isinstance(value, Count) or value > 0:
        engine.wait_ge(sem, at(value))


def settle(engine, sem):
    engine.wait_ge(sem, 1)


def build(nc, io, out):
    ctx = ExitStack()
    with ctx:
        program(nc, ctx, io, out)


def program(nc, ctx, io, out):
    def sb(name, shape, dt=F32):
        return ctx.enter_context(nc.sbuf_tensor(name, shape, dt))

    sems = {}

    def sem(name):
        if name not in sems:
            sems[name] = ctx.enter_context(nc.semaphore(name))
        return sems[name]

    X = sb("X", [P, TILES * D])
    Wqkv = sb("Wqkv", [P, 5, 3 * D], F32R)
    Wout = sb("Wout", [P, 5, D], F32R)
    W1 = sb("W1", [P, 5, FF], F32R)
    W2h = sb("W2h", [P, MC, D], F32R)
    W2l = sb("W2l", [P, MC, D], F32R)
    B2 = sb("B2", [2, D], F32R)
    rawA = sb("rawA", [P, 3, FF])
    rawC = sb("rawC", [P, MC, D])
    raw2 = sb("raw2", [2, D])
    bias = sb("bias", [32, 81])
    biasH = sb("biasH", [32, 81], F32R)
    biasL = sb("biasL", [32, 81])
    mods = [sb(f"mods{l}", [96, 6 * D], BF16) for l in range(2)]
    sel = sb("sel", [96, TILES * P], BF16)
    ident = sb("ident", [P, P])
    ones = sb("ones", [2, P], F32R)
    onesf = sb("onesf", [1, 96])
    cT = sb("cT", [96, 3, 96])
    half = sb("half", [P, 2 * 2 * H])
    gq = sb("gq", [P, HD])
    gk = sb("gk", [P, HD])
    gg = sb("gg", [P, HD])
    ys = [sb(f"ys{j}", [P, 3 * P]) for j in range(2)]
    st = [sb(f"st{j}", [P, 6]) for j in range(2)]
    mv = [sb(f"mv{j}", [P, 2]) for j in range(2)]
    ve = [sb(f"ve{j}", [P, 1]) for j in range(2)]
    rs = [sb(f"rs{j}", [P, 1]) for j in range(2)]
    yT = sb("yT", [P, 5, P], F32R)
    qks = sb("qks", [P, 2, H, SLOT], F32R)
    qT = sb("qT", [P, HP, 2, 2, N], F32R)
    kT = sb("kT", [P, HP * P], F32R)
    prob = sb("prob", [P, H * N])
    pTh = sb("pTh", [P, HP, P], FP16)
    pTl = sb("pTl", [P, HP, P], FP16)
    v1, v2, v3 = ([sb(f"v{n}{j}", [P, HP, 2 * HD + (n == 1)], BF16) for j in range(2)] for n in (1, 2, 3))
    vr = sb("vr", [P, D])
    mx = sb("mx", [P, H])
    rsum = sb("rsum", [P, 2, HP])
    os_ = sb("os", [P, 3 * P])
    oT = sb("oT", [P, 5, P], F32R)
    gate1 = sb("gate1", [P, D])
    gate2 = sb("gate2", [P, 2, D])
    c0, c1 = gate2[0:32, 0, :], gate2[0:32, 1, :]
    tmp = sb("tmp", [P, D])
    tmp2 = sb("tmp2", [P, D])
    y2T = sb("y2T", [P, 5, 2 * P], F32R)
    gl = [sb(f"gl{i}", [P, 2 * P]) for i in range(3)]
    hh = sb("hh", [P, MC, 2 * P], F32R)
    hl = sb("hl", [P, MC, 2 * P], F32R)
    shared = sb("shared", [P, 6 * D])
    adab = shared[0:1, :]
    qk, sq = (shared[:, 2 * a * D:2 * (a + 1) * D].rearrange("p (a h d) -> p a h d", a=2, h=H)
              for a in range(2))
    s1 = sb("s1", [P, 2 * H])
    s2 = sb("s2", [P, 2 * H])
    mu = sb("mu", [P, 2 * H])
    rq = sb("rq", [P, 2 * H])

    bF, bB, bM = (ctx.enter_context(nc.psum_tensor(f"bank{c}", [P, n, 512], F32)) for c, n in zip("FBM", (3, 3, 2)))

    def flat(t):
        return t[:, 0:2, :].rearrange("p a n -> p (a n)")

    t_of = lambda s, j: 2 * s + j
    col = lambda s, l, j: (s * 2 + (j - TILES * l)) * D

    S = {n: sem(n) for n in """
        x_in ada_in raw_qkv_in raw_w1_in raw_w2_in bias_in c_in g_in ada_free bias_lo_in
        zeroed sel_zero sel_made ident_zero ident_made consts pads silu_a silu_b silu_c silu_d c_turned c_copied mods_mm
        mods_a mods_b mods_c mods_d mods_e mods_f bias_h bias_l raw2_h
        wqkv_h wqkv_l wout_h wout_l w1_h w1_l w2_h w2_l
        bc1 y_turned qkv_mm q_turned ka_turned k_turned scores p_turned pv_mm o_turned proj_mm bc2 y2_turned bcg out_mm
        gate1_out yTh bcg1 qk_h v_h q_lay k_lay exps pT_h oT_h y2T_h gate2_out qk_sq
        stats aggr scaled normed spread yTl qk_l v_r v_l q_lay2 maxed shifted pT_l recip onormed ospread oT_l
        gated resid stats2 aggr2 scaled2 normed2 spread2 y2T_l gated2 resid2 qk_sum qk_mean qk_cent qk_var qk_unit
        eps1 rstd1 eps2 rstd2 v_m qk_eps qk_rstd qk_g g_made stored
    """.split()}
    h_mm = [sem(f"h_mm{c}") for c in range(MC)]
    gelu = [sem(f"gelu{c}") for c in range(MC)]
    h_hi = [sem(f"h_hi{c}") for c in range(MC)]
    h_lo = [sem(f"h_lo{c}") for c in range(MC)]

    W = {"qkv": ["L0_cond_qkv_w", "L1_cond_w_qkv"], "out": ["L0_cond_out_w", "L1_cond_w_proj"],
         "w1": ["L0_cond_w1", "L1_cond_w1"], "w2": ["L0_cond_w2", "L1_cond_w2"],
         "ada": ["L0_cond_ada_w", "L1_cond_w_mod"]}
    Bi = {"qkv": ["L0_cond_qkv_b", "L1_cond_b_qkv"], "out": ["L0_cond_out_b", "L1_cond_b_proj"],
          "w1": ["L0_cond_b1", "L1_cond_b1"], "w2": ["L0_cond_b2", "L1_cond_b2"],
          "ada": ["L0_cond_ada_b", "L1_cond_b_mod"]}
    x_rows = io["x"].rearrange("b n d -> (b n) d")
    out_rows = out.rearrange("b n d -> (b n) d")
    LAST = 2 * PAIRS
    BIAS = {"qkv": (0, 27, 0, 3 * D), "out": (27, 36, 3 * D, FF), "w1": (36, 72, 0, FF), "w2": (72, 81, 0, D)}

    def steps(engine, step, wanted, between=lambda s: None):
        step(0, 0, (0, 0), None)
        between(0)
        step(1, 0, (0, 0), 0)
        with engine.Fori(2, PAIRS - 1) as s:
            step(counts(engine, s, wanted(0)), 0, (0, 0), 0)
        step(PAIRS - 1, 0, (0, 1), 0)
        between(PAIRS - 1)
        step(PAIRS, 1, (1, 1), 0)
        between(PAIRS)
        with engine.Fori(PAIRS + 1, LAST - 1) as s:
            step(counts(engine, s, wanted(1)), 1, (1, 1), 1)
        step(LAST - 1, 1, (1, None), 1)
        step(LAST, None, (None, None), 1)

    block = ctx.enter_context(nc.Block())

    @block.sync
    def _(sp):
        def split_rows(name, l, lo, hi):
            w = io[W[name][l]]
            dmas = [(rawA[:, 0, lo:hi], w[0:P, :]), (rawA[:, 1, lo:hi], w[P:E0, :])]
            return dmas + [(rawA[32 * r:32 * r + 32, 2, lo:hi], w[E0:D, :]) for r in range(3)]

        def load_ada(l):
            w = io[W["ada"][l]].rearrange("(k p) n -> p k n", p=96)
            sp.dma_start(rawA[0:96, :, :], w[:, :, 0:FF]).then_inc(S["ada_in"], 16)
            sp.dma_start(rawC[0:96, 0:6, :].rearrange("p (k a) n -> p k (a n)", k=3),
                         w[:, :, FF:6 * D]).then_inc(S["ada_in"], 16)
            sp.dma_start(adab[:, :], io[Bi["ada"][l]].rearrange("(a n) -> a n", a=1)).then_inc(S["ada_in"], 16)

        def load_qkv_out(l):
            for name in ("qkv", "out"):
                lo, hi = BIAS[name][2:]
                for dst, src in split_rows(name, l, lo, hi):
                    sp.dma_start(dst, src).then_inc(S["raw_qkv_in"], 16)
                sp.dma_start(rawA[96:97, 2, lo:hi], io[Bi[name][l]].rearrange("(a n) -> a n", a=1))\
                    .then_inc(S["raw_qkv_in"], 16)
                sp.dma_start(rawA[97:98, 2, lo:hi], biasL[:, BIAS[name][0]:BIAS[name][1]])\
                    .then_inc(S["raw_qkv_in"], 16)

        def load_w1(l):
            for dst, src in split_rows("w1", l, 0, FF):
                sp.dma_start(dst, src).then_inc(S["raw_w1_in"], 16)
            sp.dma_start(rawA[96:97, 2, :], io[Bi["w1"][l]].rearrange("(a n) -> a n", a=1)).then_inc(S["raw_w1_in"], 16)
            sp.dma_start(rawA[97:98, 2, :], biasL[:, BIAS["w1"][0]:BIAS["w1"][1]]).then_inc(S["raw_w1_in"], 16)

        def load_w2(l):
            sp.dma_start(rawC[:, :, :], io[W["w2"][l]].rearrange("(c p) n -> p c n", p=P)).then_inc(S["raw_w2_in"], 16)
            sp.dma_start(raw2[0:1, :], io[Bi["w2"][l]].rearrange("(a n) -> a n", a=1)).then_inc(S["raw_w2_in"], 16)
            sp.dma_start(raw2[1:2, :], biasL[:, BIAS["w2"][0]:BIAS["w2"][1]]).then_inc(S["raw_w2_in"], 16)

        def load_bias(l):
            for name in ("qkv", "out", "w1", "w2"):
                a, b = BIAS[name][0:2]
                sp.dma_start(bias[:, a:b], io[Bi[name][l]].rearrange("(p n) -> p n", p=32)).then_inc(S["bias_in"], 16)

        sp.dma_start(c0[:, :], io["cond_1152"]).then_inc(S["c_in"], 16)
        load_ada(0)
        load_bias(0)
        for g in range(4):
            sp.dma_start(X[:, g * 4 * D:(g + 1) * 4 * D].rearrange("p (t d) -> p t d", t=4),
                         x_rows[g * 4 * P:(g + 1) * 4 * P, :].rearrange("(t p) d -> p t d", p=P))\
                .then_inc(S["x_in"], 16)
        for dst, name in ((gq, "L1_cond_g_q"), (gk, "L1_cond_g_k")):
            sp.dma_start(dst[:, :], io[name].rearrange("(a n) -> a n", a=1).to_broadcast([P, HD])).then_inc(S["g_in"], 16)
        for l in range(2):
            if l:
                sp.wait_ge(S["w1_h"], 2 * l - 1)
                sp.wait_ge(S["w1_l"], 2 * l - 1)
                sp.wait_ge(S["w2_h"], 2 * l - 1)
                sp.wait_ge(S["w2_l"], 2 * l - 1)
                load_ada(l)
                sp.wait_ge(S["bias_l"], l)
                load_bias(l)
            sp.wait_ge(S["mods_mm"], 2 * l + 2)
            sp.wait_ge(S["bias_l"], l + 1)
            if l == 0:
                sp.wait_ge(S["zeroed"], 1)
            load_qkv_out(l)
            load_w2(l)
            for split in ("wqkv_h", "wqkv_l", "wout_h", "wout_l"):
                sp.wait_ge(S[split], l + 1)
            load_w1(l)

        def store(s):
            for j in range(2):
                sp.wait_ge(S["resid2"], at(t_of(s, j) - 1))
                sp.dma_start(out_rows[bass.ds(at((s * 2 + (j - TILES - 2)) * P), P), :],
                             X[:, bass.ds(at(col(s, 1, j - 2)), D)]).then_inc(S["stored"], 16)

        with sp.Fori(PAIRS + 1, LAST + 1) as s:
            store(counts(sp, s, [(2, -1), (2, 0)] + [(2 * w, (j - TILES - 2) * w) for w in (D, P) for j in range(2)]))
        sp.wait_ge(S["stored"], 16 * TILES)

    @block.gpsimd
    def _(pool):
        pool.memset(rawA[96:128, 2, :], 0.0).then_inc(S["zeroed"], 1)
        pool.wait_ge(S["zeroed"], 1)
        pool.memset(ident[:, :], 0.0).then_inc(S["ident_zero"], 1)
        pool.wait_ge(S["ident_zero"], 1)
        pool.affine_select(out=ident[:, :], in_=ident[:, :], compare_op=ALU.not_equal, fill=1.0, base=0,
                           pattern=[[-1, P]], channel_multiplier=1).then_inc(S["ident_made"], 1)
        pool.wait_ge(S["ident_made"], 1)
        pool.memset(sel[:, :], 0.0).then_inc(S["sel_zero"], 1)
        pool.wait_ge(S["sel_zero"], 1)
        seq = sel[:, :].rearrange("p (m n) -> p m n", n=N)
        for g in range(3):
            pool.affine_select(out=seq, in_=seq, compare_op=ALU.not_equal, fill=1.0, base=-32 * g,
                               pattern=[[-1, B], [0, N]], channel_multiplier=1).then_inc(S["sel_made"], 1)
            pool.wait_ge(S["sel_made"], g + 1)
        pool.wait_ge(S["g_in"], 32)
        pool.tensor_tensor(gg[:, :], gq[:, :], gk[:, :], ALU.mult).then_inc(S["g_made"], 1)

        def row_scale(t, n, eps_sem, out_sem, var_sem):
            settle(pool, S["consts"])
            pool.wait_ge(var_sem, at(t + 1))
            pool.tensor_scalar(ve[n][:, :], mv[n][:, 1:2], EPS, None, ALU.add).then_inc(eps_sem, 1)
            pool.wait_ge(eps_sem, at(t + 1))
            pool.tensor_tensor(rs[n][:, :], ve[n][:, :], half[:, 0:1], ALU.pow).then_inc(out_sem, 1)

        def head_scale(t):
            settle(pool, S["consts"])
            pool.wait_ge(S["qk_var"], at(t + 1))
            pool.tensor_scalar(s2[:, :], s2[:, :], 1.0 / HD, EPS, ALU.mult, ALU.add).then_inc(S["qk_eps"], 1)
            pool.wait_ge(S["qk_eps"], at(t + 1))
            pool.tensor_tensor(rq[:, :], s2[:, :], half[:, 0:2 * H], ALU.pow).then_inc(S["qk_rstd"], 1)

        def value_mid(t, p):
            settle(pool, S["consts"])
            pool.wait_ge(S["v_r"], at(t + 1))
            previous(pool, S["pv_mm"], t - 1)
            pool.tensor_scalar(v2[p][:, :, :], vr[:, :].rearrange("p (a n) -> p a n", a=HP), 1.0, 0.0,
                               ALU.mult, ALU.add).then_inc(S["v_m"], 1)

        def hidden(s, c):
            settle(pool, S["consts"])
            pool.wait_ge(gelu[c], at(s))
            previous(pool, S["out_mm"], t_of(s, -2))
            pool.tensor_scalar(hh[:, c, :], gl[c % 3][:, :], 1.0, 0.0, ALU.mult, ALU.add).then_inc(h_hi[c], 1)
            pool.wait_ge(h_hi[c], at(s))
            pool.tensor_tensor(hl[:, c, :], gl[c % 3][:, :], hh[:, c, :].bitcast(F32), ALU.subtract)\
                .then_inc(h_lo[c], 1)

        def step(s, back, front, mlp):
            h = lambda *cs: [hidden(s, c) for c in cs if mlp is not None]
            for j in range(2):
                if front[j] is not None:
                    row_scale(t_of(s, j + 1), 0, S["eps1"], S["rstd1"], S["aggr"])
                if j == 0:
                    h(0, 1, 2)
                if front[j] is not None:
                    value_mid(t_of(s, j + 1), (j + 1) % 2)
                    if front[j] == 1:
                        head_scale(t_of(s, j + 1) - TILES)
                if j == 0:
                    h(3, 4, 5)
                if back is not None:
                    row_scale(t_of(s, j), 1, S["eps2"], S["rstd2"], S["aggr2"])
                if j == 0:
                    h(6, 7, 8)

        def wanted(l):
            return [(1, 0), (2, -2), (2, 0), (2, 1), (2, 2), (2, 3)] + [(2, n - TILES) for n in (1, 2, 3)] * l

        pool.wait_ge(S["consts"], 1)
        row_scale(0, 0, S["eps1"], S["rstd1"], S["aggr"])
        value_mid(0, 0)
        steps(pool, step, wanted)

    @block.scalar
    def _(act):
        def cast(dst, src, sem=None):
            i = act.activation(dst, src, ACT.Copy)
            return i.then_inc(sem, 1) if sem is not None else i

        def weights_qkv(l):
            act.wait_ge(S["raw_qkv_in"], 16 * 14 * (l + 1))
            previous(act, S["qkv_mm"], TILES * l)
            for k in range(3):
                i = cast(Wqkv[:, k, :], rawA[:, k, 0:3 * D])
            i.then_inc(S["wqkv_h"], 1)

        def weights_out(l):
            previous(act, S["proj_mm"], TILES * l)
            cast(Wout[:, 0:3, :], rawA[:, :, 3 * D:FF], S["wout_h"])

        def weights_mlp(l):
            act.wait_ge(S["raw_w1_in"], 16 * 7 * (l + 1))
            previous(act, h_mm[MC - 1], PAIRS * l)
            for k in range(3):
                i = cast(W1[:, k, :], rawA[:, k, :])
            i.then_inc(S["w1_h"], 1)
            act.wait_ge(S["raw_w2_in"], 16 * 3 * (l + 1))
            previous(act, S["out_mm"], TILES * l)
            cast(B2[:, :], raw2[:, :])
            cast(W2h[:, :, :], rawC[:, :, :], S["w2_h"])

        def high_bias(l):
            act.wait_ge(S["bias_in"], 64 * (l + 1))
            previous(act, S["bias_l"], l)
            cast(biasH[:, :], bias[:, :], S["bias_h"])

        def gate_one(t):
            act.wait_ge(S["bcg1"], at(t + 1))
            previous(act, S["gated"], t)
            cast(gate1[:, :], bB[:, 2, 0:D], S["gate1_out"])

        def turned_y(t):
            act.wait_ge(S["y_turned"], at(t + 1))
            previous(act, S["qkv_mm"], t)
            cast(yT[:, 0:3, :], bF[:, 2, 0:3 * P].rearrange("p (k n) -> p k n", k=3), S["yTh"])

        def split_v(t, l, p):
            act.wait_ge(S["qkv_mm"], at(t + 1))
            previous(act, S["pv_mm"], t - 1)
            cast(v1[p][:, :, 0:2 * HD], bF[:, 2, 0:D].rearrange("p (a n) -> p a n", a=HP), S["v_h"])
            if l:
                act.wait_ge(S["qk_cent"], at(t + 1 - TILES))
                act.activation(sq[:, :, :, :], qk[:, :, :, :], ACT.Square).then_inc(S["qk_sq"], 1)

        def split_qk(t, l):
            previous(act, S["k_turned"], t)
            if l:
                act.wait_ge(S["qk_g"], at(t + 1 - TILES))
                q, k = qk[:, 0, :, :], qk[:, 1, :, :]
            else:
                act.wait_ge(S["qkv_mm"], at(t + 1))
                q, k = (bF[:, a, 0:D].rearrange("p (h d) -> p h d", h=H) for a in range(2))
            cast(qks[:, 0, :, 0:HD], q)
            cast(qks[:, 0, :, 2 * HD:3 * HD], q)
            cast(qks[:, 1, :, 0:HD], k)
            cast(qks[:, 1, :, HD:2 * HD], k, S["qk_h"])

        def lay_qk(t):
            act.wait_ge(S["q_turned"], at(t + 1))
            previous(act, S["scores"], t)
            cast(qT[0:64, :, :, 0, :], flat(bF)[0:64, :].rearrange("p (a b q) -> p a b q", a=HP, b=2), S["q_lay"])
            act.wait_ge(S["ka_turned"], at(t + 1))
            cast(kT[:, 0:512], bF[:, 2, :])
            act.wait_ge(S["k_turned"], at(t + 1))
            cast(kT[:, 512:1024], bF[:, 0, :], S["k_lay"])

        def exp(t):
            act.wait_ge(S["shifted"], at(t + 1))
            act.activation(prob[:, :], prob[:, :], ACT.Exp, scale=SCALE).then_inc(S["exps"], 1)

        def turned_p(t):
            act.wait_ge(S["p_turned"], at(t + 1))
            previous(act, S["pv_mm"], t)
            cast(pTh[:, :, :], flat(bB).rearrange("p (a n) -> p a n", a=HP), S["pT_h"])

        def turned_o(t):
            act.wait_ge(S["o_turned"], at(t + 1))
            previous(act, S["proj_mm"], t)
            cast(oT[:, 0:3, :], bB[:, 2, 0:3 * P].rearrange("p (k n) -> p k n", k=3), S["oT_h"])

        def turned_y2(s, j):
            t = t_of(s, j)
            act.wait_ge(S["y2_turned"], at(t + 1))
            previous(act, h_mm[MC - 1], s)
            cast(y2T[:, 0:3, j * P:(j + 1) * P], bB[:, 2, 0:3 * P].rearrange("p (k n) -> p k n", k=3), S["y2T_h"])

        def gate_two(s):
            act.wait_ge(S["bcg"], at(s))
            previous(act, S["gated2"], t_of(s, -2))
            cast(gate2[:, :, :], bM[:, :, 0:D], S["gate2_out"])

        def hidden(s, c):
            act.wait_ge(h_mm[c], at(s))
            if c >= 3:
                act.wait_ge(h_lo[c - 3], at(s))
            else:
                previous(act, h_lo[MC - 3 + c], s - 1)
            act.activation(gl[c % 3][:, :], bM[:, c % 2, 0:2 * P], ACT.Gelu_apprx_tanh).then_inc(gelu[c], 1)

        def step(s, back, front, mlp):
            g = lambda *cs: [hidden(s, c) for c in cs if mlp is not None]
            if mlp is not None:
                gate_two(s)
            if back is None:
                g(*range(MC))
                return
            for j in range(2):
                t, f = t_of(s, j), front[j]
                h = g if j == 0 else (lambda *cs: None)
                gate_one(t)
                exp(t)
                if f is not None:
                    turned_y(t + 1)
                h(0)
                turned_p(t)
                h(1)
                if f is not None:
                    if f == 1 and not isinstance(s, Count) and s == PAIRS - 1:
                        weights_qkv(1)
                    split_v(t + 1, f, (j + 1) % 2)
                    if f == 0:
                        split_qk(t + 1, f)
                h(2, 3)
                turned_o(t)
                if f == 1:
                    split_qk(t + 1, f)
                h(4)
                if f is not None:
                    lay_qk(t + 1)
                h(5, 6)
                turned_y2(s, j)
                h(7, 8)

        def wanted(l):
            return [(1, 0), (1, -1), (2, -2), (2, -1), (2, 0), (2, 1), (2, 2), (2, 3)] + \
                [(2, n - TILES) for n in (1, 2, 3)] * l

        def between(s):
            if s == 0:
                high_bias(1)
            elif s == PAIRS - 1:
                weights_out(1)
            elif s == PAIRS:
                weights_mlp(1)

        act.wait_ge(S["c_in"], 16)
        act.activation(c1[:, :], c0[:, :], ACT.Exp, scale=-1.0).then_inc(S["silu_a"], 1)
        high_bias(0)
        weights_qkv(0)
        weights_out(0)
        turned_y(0)
        split_v(0, 0, 0)
        split_qk(0, 0)
        lay_qk(0)
        weights_mlp(0)
        steps(act, step, wanted, between)

    @block.tensor
    def _(pe):
        def product(outs, stationary, moving, sem):
            for n, (a, b) in enumerate(PASSES):
                for o, cols in outs:
                    i = pe.matmul(o, stationary[:, a, :], moving[:, b, cols], start=(n == 0),
                                  stop=(n == len(PASSES) - 1), skip_group_check=True)
            i.then_inc(sem, 1)

        def turn_three(dst, src, sem):
            for k in range(3):
                i = pe.transpose(dst[:, k * P:(k + 1) * P], src[:, k * P:(k + 1) * P], ident[:, :])
            i.then_inc(sem, 1)

        def modulation(l):
            pe.wait_ge(S["ada_in"], 48 * (l + 1))
            for part in range(2):
                if l or part:
                    pe.wait_ge(S["mods_a"], 2 * l + part)
                for m in range(3):
                    b = bF[0:96, m, 0:D]
                    for k in range(3):
                        c = (3 * part + m) * D
                        w = rawA[0:96, k, c:c + D] if c < FF else \
                            rawC[0:96, 2 * k + (c - FF) // D, :]
                        pe.matmul(b, cT[:, k, :], w, start=(k == 0), stop=False)
                    i = pe.matmul(b, onesf[:, :], adab[:, c:c + D], start=False, stop=True)
                i.then_inc(S["mods_mm"], 1)

        def spread(s, l, j, which, dst):
            tile = bass.ds(at((s * 2 + (j - TILES * l)) * P), P)
            for m, d in zip(which, dst):
                i = pe.matmul(d, sel[:, tile], mods[l][:, m * D:(m + 1) * D], start=True, stop=True)
            return i

        def spread_one(s, l, j):
            t = t_of(s, j)
            previous(pe, S["k_lay"], t)
            previous(pe, S["q_lay"], t)
            previous(pe, S["q_lay2"], t)
            spread(s, l, j, (SCALE1, SHIFT1), (bF[:, 0, 0:D], bF[:, 1, 0:D])).then_inc(S["bc1"], 1)

        def spread_gate1(s, l, j):
            t = t_of(s, j)
            previous(pe, S["y2T_l"], t)
            previous(pe, S["y2T_h"], t)
            spread(s, l, j, (GATE1,), (bB[:, 2, 0:D],)).then_inc(S["bcg1"], 1)

        def turn_y(t):
            pe.wait_ge(S["spread"], at(t + 1))
            turn_three(bF[:, 2, :], ys[0], S["y_turned"])

        def qkv(t):
            pe.wait_ge(S["yTh"], at(t + 1))
            pe.wait_ge(S["yTl"], at(t + 1))
            product([(bF[:, m, 0:D], slice(m * D, (m + 1) * D)) for m in range(3)], yT, Wqkv, S["qkv_mm"])

        def turn_qk(t):
            pe.wait_ge(S["qk_h"], at(t + 1))
            pe.wait_ge(S["qk_l"], at(t + 1))
            turn_pairs(0, range(HP), flat(bF), S["q_turned"])
            pe.wait_ge(S["v_r"], at(t + 1))
            pe.wait_ge(S["v_h"], at(t + 1))
            turn_pairs(1, range(HP // 2), bF[:, 2, :], S["ka_turned"])

        def turn_k(t):
            pe.wait_ge(S["q_lay"], at(t + 1))
            pe.wait_ge(S["q_lay2"], at(t + 1))
            turn_pairs(1, range(HP // 2, HP), bF[:, 0, :], S["k_turned"])

        def turn_pairs(which, pairs, dst, done):
            src = qks[:, which, :, :].rearrange("p h c -> p (h c)").bitcast(F32)
            for n, a in enumerate(pairs):
                i = pe.transpose(dst[:, n * P:(n + 1) * P], src[:, a * P:(a + 1) * P], ident[:, :])
            i.then_inc(done, 1)

        def scores(t):
            pe.wait_ge(S["q_lay"], at(t + 1))
            pe.wait_ge(S["q_lay2"], at(t + 1))
            pe.wait_ge(S["k_lay"], at(t + 1))
            previous(pe, S["normed2"], t)
            for a in range(HP):
                for b in range(2):
                    c = (2 * a + b) * N
                    i = pe.matmul(flat(bB)[:, c:c + N], qT[:, a, b, :, :].rearrange("p h q -> p (h q)"),
                                  kT[:, a * P + b * N:a * P + (b + 1) * N], start=True, stop=True)
            i.then_inc(S["scores"], 1)

        def turn_p(t):
            pe.wait_ge(S["exps"], at(t + 1))
            for a in range(HP):
                i = pe.transpose(flat(bB)[:, a * P:(a + 1) * P], prob[:, a * P:(a + 1) * P], ident[:, :])
            i.then_inc(S["p_turned"], 1)

        def pv(t, par):
            pe.wait_ge(S["pT_h"], at(t + 1))
            pe.wait_ge(S["pT_l"], at(t + 1))
            pe.wait_ge(S["v_l"], at(t + 1))
            pe.wait_ge(S["v_m"], at(t + 1))
            for a in range(HP):
                for n, (p, v) in enumerate(((pTh, v1[par]), (pTh, v2[par]), (pTh, v3[par]), (pTl, v1[par]), (pTl, v2[par]))):
                    for b in range(2):
                        rows = slice(b * N, (b + 1) * N)
                        w = v.shape[2]
                        c = a * (2 * HD + 1)
                        i = pe.matmul(bB[:, b, c:c + w], p[rows, a, :], v[rows, a, :], start=(n == 0),
                                      stop=(n == 4), skip_group_check=True)
            i.then_inc(S["pv_mm"], 1)

        def turn_o(t):
            pe.wait_ge(S["ospread"], at(t + 1))
            pe.wait_ge(S["gate1_out"], at(t + 1))
            turn_three(bB[:, 2, :], os_, S["o_turned"])

        def project(t):
            pe.wait_ge(S["oT_h"], at(t + 1))
            pe.wait_ge(S["oT_l"], at(t + 1))
            product([(bB[:, 2, 0:D], slice(0, D))], oT, Wout, S["proj_mm"])

        def spread_two(s, l, j):
            pe.wait_ge(S["onormed"], at(t_of(s, j) + 1))
            spread(s, l, j, (SCALE2, SHIFT2), (bB[:, 0, 0:D], bB[:, 1, 0:D])).then_inc(S["bc2"], 1)

        def turn_y2(t):
            pe.wait_ge(S["spread2"], at(t + 1))
            turn_three(bB[:, 2, :], ys[1], S["y2_turned"])

        def spread_gate(s, l):
            previous(pe, S["gated2"], t_of(s, -2))
            for j in range(2):
                i = spread(s, l, j - 2, (GATE2,), (bM[:, j, 0:D],))
            i.then_inc(S["bcg"], 1)

        def hidden(s, c):
            if c == 0:
                pe.wait_ge(S["y2T_h"], at(t_of(s, 0)))
                pe.wait_ge(S["y2T_l"], at(t_of(s, 0)))
            if c < 2:
                pe.wait_ge(S["gate2_out"], at(s))
            else:
                pe.wait_ge(gelu[c - 2], at(s))
            for n, (a, b) in enumerate(PASSES):
                i = pe.matmul(bM[:, c % 2, 0:2 * P], W1[:, a, c * P:(c + 1) * P], y2T[:, b, :],
                              start=(n == 0), stop=(n == len(PASSES) - 1))
            i.then_inc(h_mm[c], 1)

        def second(s, j, chunks):
            o = bM[:, j, 0:D]
            for c in chunks:
                if c == 0:
                    pe.wait_ge(gelu[MC - 1], at(s))
                    if j:
                        pe.wait_ge(gelu[MC - 2], at(s))
                    pe.matmul(o, ones[:, :], B2[:, :], start=True, stop=False)
                if j == 0:
                    pe.wait_ge(h_hi[c], at(s))
                    pe.wait_ge(h_lo[c], at(s))
                tile = slice(j * P, (j + 1) * P)
                for hid, w in ((hh, W2h), (hh, W2l), (hl, W2h)):
                    i = pe.matmul(o, hid[:, c, tile], w[:, c, :], start=False,
                                  stop=(c == MC - 1 and w is W2h and hid is hl))
                if c == MC - 1:
                    i.then_inc(S["out_mm"], 1)

        def step(s, back, front, mlp):
            m1 = lambda *cs: [hidden(s, c) for c in cs if mlp is not None]
            m2 = lambda j, *cs: second(s, j, cs) if mlp is not None else None
            if mlp is not None:
                spread_gate(s, mlp)
            if back is None:
                m1(*range(MC))
                m2(0, *range(MC))
                m2(1, *range(MC))
                return
            for j in range(2):
                t, f = t_of(s, j), front[j]
                fill = lambda first, then: first() if j == 0 else then()
                scores(t)
                spread_gate1(s, back, j)
                if f is not None:
                    spread_one(s, f, j + 1)
                fill(lambda: m1(0, 1), lambda: m2(0, 0, 1, 2))
                if f is not None:
                    turn_y(t + 1)
                fill(lambda: None, lambda: m2(0, 3))
                turn_p(t)
                fill(lambda: m1(2), lambda: m2(0, 4))
                if f is not None:
                    if not isinstance(s, Count) and t == TILES - 1:
                        pe.wait_ge(S["wqkv_h"], 2)
                        pe.wait_ge(S["wqkv_l"], 2)
                    qkv(t + 1)
                if not isinstance(s, Count) and s == 0 and j == 0:
                    pe.wait_ge(S["consts"], 1)
                pv(t, j)
                fill(lambda: m1(3, 4), lambda: m2(0, 5, 6))
                turn_o(t)
                if f == 0:
                    turn_qk(t + 1)
                fill(lambda: m1(5), lambda: m2(0, 7, 8))
                if not isinstance(s, Count) and j == 0 and s in (0, PAIRS):
                    pe.wait_ge(S["wout_h"], s // PAIRS + 1)
                    pe.wait_ge(S["wout_l"], s // PAIRS + 1)
                project(t)
                spread_two(s, back, j)
                fill(lambda: m1(6), lambda: m2(1, 0, 1, 2))
                if f == 1:
                    turn_qk(t + 1)
                fill(lambda: None, lambda: m2(1, 3, 4))
                if f is not None:
                    turn_k(t + 1)
                fill(lambda: m1(7), lambda: m2(1, 5, 6))
                turn_y2(t)
                fill(lambda: m1(8), lambda: m2(1, 7, 8))

        def wanted(l):
            tiles = [(2 * P, (j - TILES * l) * P) for j in (-2, -1, 0, 1, 2)]
            return [(1, 0), (2, -2), (2, -1), (2, 0), (2, 1), (2, 2), (2, 3)] + tiles

        def between(s):
            if s == 0:
                for laid in ("k_lay", "q_lay", "q_lay2"):
                    pe.wait_ge(S[laid], 3)
                modulation(1)
                pe.wait_ge(S["mods_a"], 4)
            if s in (0, PAIRS):
                for split in ("w1_h", "w1_l", "w2_h", "w2_l"):
                    pe.wait_ge(S[split], s // PAIRS + 1)

        pe.wait_ge(S["ident_made"], 1)
        pe.wait_ge(S["silu_d"], 1)
        for k in range(3):
            i = pe.transpose(bB[0:96, 2, k * 32:(k + 1) * 32], c0[:, k * 96:(k + 1) * 96], ident[0:32, 0:32])
        i.then_inc(S["c_turned"], 1)
        pe.wait_ge(S["c_copied"], 1)
        pe.wait_ge(S["consts"], 1)
        pe.wait_ge(S["sel_made"], 3)
        modulation(0)
        pe.wait_ge(S["mods_f"], 2)
        spread_one(0, 0, 0)
        turn_y(0)
        pe.wait_ge(S["wqkv_h"], 1)
        pe.wait_ge(S["wqkv_l"], 1)
        pe.wait_ge(S["pads"], 1)
        qkv(0)
        turn_qk(0)
        turn_k(0)
        steps(pe, step, wanted, between)

    @block.vector
    def _(dve):
        def weights_qkv(l):
            dve.wait_ge(S["wqkv_h"], l + 1)
            dve.tensor_tensor(Wqkv[:, AL:BL + 1, :], rawA[:, 0:2, 0:3 * D], Wqkv[:, A:BB + 1, :].bitcast(F32), ALU.subtract)
            dve.tensor_tensor(Wqkv[64:96, E, :], rawA[64:96, 2, 0:3 * D], Wqkv[64:96, E, :].bitcast(F32), ALU.subtract)\
                .then_inc(S["wqkv_l"], 1)

        def weights_out(l):
            dve.wait_ge(S["wout_h"], l + 1)
            dve.tensor_tensor(Wout[:, AL:BL + 1, :], rawA[:, 0:2, 3 * D:FF], Wout[:, A:BB + 1, :].bitcast(F32), ALU.subtract)
            dve.tensor_tensor(Wout[64:96, E, :], rawA[64:96, 2, 3 * D:FF], Wout[64:96, E, :].bitcast(F32), ALU.subtract)\
                .then_inc(S["wout_l"], 1)

        def weights_mlp(l):
            dve.wait_ge(S["w1_h"], l + 1)
            dve.tensor_tensor(W1[:, AL:BL + 1, :], rawA[:, 0:2, :], W1[:, A:BB + 1, :].bitcast(F32), ALU.subtract)
            dve.tensor_tensor(W1[64:96, E, :], rawA[64:96, 2, :], W1[64:96, E, :].bitcast(F32), ALU.subtract)\
                .then_inc(S["w1_l"], 1)
            dve.wait_ge(S["w2_h"], l + 1)
            dve.tensor_tensor(W2l[:, :, :], rawC[:, :, :], W2h[:, :, :].bitcast(F32), ALU.subtract).then_inc(S["w2_l"], 1)

        def modulation(l):
            for part in range(2):
                n = 2 * l + part + 1
                m = mods[l][:, 3 * part * D:3 * (part + 1) * D]
                full = prob[0:96, 0:3 * D]
                dve.wait_ge(S["mods_mm"], n)
                previous(dve, S["mods_f"], n - 1)
                dve.tensor_scalar(prob[0:96, 0:D], bF[0:96, 0, 0:D], 0.0, None, ALU.add)
                dve.tensor_scalar(prob[0:96, D:2 * D], bF[0:96, 1, 0:D], 1.0, None, ALU.add)
                dve.tensor_scalar(prob[0:96, 2 * D:3 * D], bF[0:96, 2, 0:D], 0.0, None, ALU.add).then_inc(S["mods_a"], 1)
                dve.wait_ge(S["mods_a"], n)
                dve.tensor_copy(m, full).then_inc(S["mods_b"], 1)
                dve.wait_ge(S["mods_b"], n)
                for r in (32, 64):
                    i = dve.tensor_tensor(prob[r:r + 32, 0:3 * D], prob[r:r + 32, 0:3 * D], m[r:r + 32, :], ALU.subtract)
                i.then_inc(S["mods_c"], 1)
                dve.wait_ge(S["mods_c"], n)
                for r in (32, 64):
                    i = dve.tensor_copy(m[r:r + 32, :], prob[r:r + 32, 0:3 * D])
                i.then_inc(S["mods_d"], 1)
                dve.wait_ge(S["mods_d"], n)
                dve.tensor_tensor(prob[64:96, 0:3 * D], prob[64:96, 0:3 * D], m[64:96, :], ALU.subtract).then_inc(S["mods_e"], 1)
                dve.wait_ge(S["mods_e"], n)
                dve.tensor_copy(m[64:96, :], prob[64:96, 0:3 * D]).then_inc(S["mods_f"], 1)

        def low_bias(l):
            dve.wait_ge(S["bias_h"], l + 1)
            if l:
                dve.wait_ge(S["w1_h"], 1)
                dve.wait_ge(S["w2_h"], 1)
            dve.tensor_tensor(biasL[:, :], bias[:, :], biasH[:, :].bitcast(F32), ALU.subtract).then_inc(S["bias_l"], 1)

        def moments(s, l, j, n, sems):
            t = t_of(s, j)
            stats, aggr = sems[0:2]
            dve.bn_stats(st[n][:, :], X[:, bass.ds(at(col(s, l, j)), D)]).then_inc(stats, 1)
            settle(dve, S["silu_a"])
            dve.wait_ge(stats, at(t + 1))
            dve.bn_aggr(mv[n][:, :], st[n][:, :]).then_inc(aggr, 1)

        def norm(s, l, j, n, sems):
            t = t_of(s, j)
            aggr, rstd, bc, scaled, normed, repeated = sems[1:]
            x, y, b = X[:, bass.ds(at(col(s, l, j)), D)], ys[n], (bF, bB)[n]
            dve.wait_ge(aggr, at(t + 1))
            dve.wait_ge(bc, at(t + 1))
            dve.scalar_tensor_tensor(y[:, 0:D], x, mv[n][:, 0:1], b[:, 0, 0:D], ALU.subtract, ALU.mult).then_inc(scaled, 1)
            dve.wait_ge(scaled, at(t + 1))
            dve.wait_ge(rstd, at(t + 1))
            dve.scalar_tensor_tensor(y[:, 0:D], y[:, 0:D], rs[n][:, 0:1], b[:, 1, 0:D], ALU.mult, ALU.add).then_inc(normed, 1)
            dve.wait_ge(normed, at(t + 1))
            dve.tensor_copy(y[:, D:D + 2 * TAIL].rearrange("p (a n) -> p a n", a=2),
                            y[:, E0:D].unsqueeze(1).to_broadcast([P, 2, TAIL])).then_inc(repeated, 1)

        norm1 = [S[n] for n in "stats aggr rstd1 bc1 scaled normed spread".split()]
        norm2 = [S[n] for n in "stats2 aggr2 rstd2 bc2 scaled2 normed2 spread2".split()]

        def moments_one(s, l, j):
            t = t_of(s, j)
            settle(dve, S["silu_a"])
            if not isinstance(s, Count):
                dve.wait_ge(S["x_in"], 64)
            previous(dve, S["resid2"], t - TILES + 1 if l else 0)
            moments(s, l, j, 0, norm1)

        def norm_one(s, l, j):
            previous(dve, S["y_turned"], t_of(s, j))
            norm(s, l, j, 0, norm1)

        def low(dst, turned, sem, hi_sem, n):
            dve.wait_ge(hi_sem, at(n))
            dve.tensor_tensor(dst[:, AL:BL + 1, :], turned[:, 0:2, :], dst[:, A:BB + 1, :].bitcast(F32), ALU.subtract)
            dve.tensor_tensor(dst[32:64, E, :], turned[32:64, 2, :], dst[32:64, E, :].bitcast(F32), ALU.subtract)\
                .then_inc(sem, 1)

        def turned(bank_):
            return bank_[:, 2, 0:3 * P].rearrange("p (k n) -> p k n", k=3)

        def head_norm(t):
            u = t - TILES
            z = bF[:, 0:2, 0:D].rearrange("p a (h d) -> p a h d", h=H)
            heads = lambda a: a[:, :].rearrange("p (a h) -> p a h", a=2).unsqueeze(3).to_broadcast([P, 2, H, HD])
            dve.wait_ge(S["qkv_mm"], at(t + 1))
            dve.tensor_reduce(s1[:, :].rearrange("p (a h) -> p a h", a=2), z, AX.X, ALU.add).then_inc(S["qk_sum"], 1)
            dve.wait_ge(S["qk_sum"], at(u + 1))
            dve.tensor_scalar(mu[:, :], s1[:, :], 1.0 / HD, None, ALU.mult).then_inc(S["qk_mean"], 1)
            dve.wait_ge(S["qk_mean"], at(u + 1))
            for read in (S["qk_h"], S["qk_l"]):
                previous(dve, read, t if isinstance(t, Count) or t > TILES else 0)
            for a in range(2):
                i = dve.tensor_tensor(qk[:, a, :, :], z[:, a, :, :], heads(mu)[:, a, :, :], ALU.subtract)
            i.then_inc(S["qk_cent"], 1)
            dve.wait_ge(S["qk_sq"], at(u + 1))
            dve.tensor_reduce(s2[:, :].rearrange("p (a h) -> p a h", a=2), sq[:, :, :, :], AX.X, ALU.add).then_inc(S["qk_var"], 1)

        def head_norm_end(t):
            u = t - TILES
            heads = lambda a: a[:, :].rearrange("p (a h) -> p a h", a=2).unsqueeze(3).to_broadcast([P, 2, H, HD])
            dve.wait_ge(S["qk_rstd"], at(u + 1))
            for a in range(2):
                i = dve.tensor_tensor(qk[:, a, :, :], qk[:, a, :, :], heads(rq)[:, a, :, :], ALU.mult)
            i.then_inc(S["qk_unit"], 1)
            dve.wait_ge(S["qk_unit"], at(u + 1))
            dve.tensor_tensor(qk[:, 0, :, :], qk[:, 0, :, :], gg[:, :].unsqueeze(1).to_broadcast([P, H, HD]), ALU.mult)\
                .then_inc(S["qk_g"], 1)

        def split_v(t, p):
            dve.wait_ge(S["v_h"], at(t + 1))
            v = bF[:, 2, 0:D].rearrange("p (a n) -> p a n", a=HP)
            r = vr[:, :].rearrange("p (a n) -> p a n", a=HP)
            previous(dve, S["v_l"], t)
            dve.tensor_tensor(r, v, v1[p][:, :, 0:2 * HD], ALU.subtract).then_inc(S["v_r"], 1)

        def split_qk(t, l, p):
            dve.wait_ge(S["qk_h"], at(t + 1))
            if l == 0:
                q, k = (bF[:, a, 0:D].rearrange("p (h d) -> p h d", h=H) for a in range(2))
            else:
                q, k = qk[:, 0, :, :], qk[:, 1, :, :]
            dve.tensor_tensor(qks[:, 0, :, HD:2 * HD], q, qks[:, 0, :, 0:HD].bitcast(F32), ALU.subtract)
            dve.tensor_tensor(qks[:, 1, :, 2 * HD:3 * HD], k, qks[:, 1, :, 0:HD].bitcast(F32), ALU.subtract).then_inc(S["qk_l"], 1)
            dve.wait_ge(S["v_m"], at(t + 1))
            dve.tensor_tensor(v3[p][:, :, :], vr[:, :].rearrange("p (a n) -> p a n", a=HP), v2[p][:, :, :], ALU.subtract)\
                .then_inc(S["v_l"], 1)

        def lay_q(t):
            dve.wait_ge(S["q_turned"], at(t + 1))
            previous(dve, S["scores"], t)
            dve.tensor_copy(qT[64:128, :, :, 1, :], flat(bF)[64:128, :].rearrange("p (a b q) -> p a b q", a=HP, b=2))\
                .then_inc(S["q_lay2"], 1)

        def softmax(t):
            z = flat(bB).rearrange("p (a n) -> p a n", n=N)
            dve.wait_ge(S["scores"], at(t + 1))
            dve.tensor_reduce(mx[:, :], z, AX.X, ALU.max).then_inc(S["maxed"], 1)
            dve.wait_ge(S["maxed"], at(t + 1))
            previous(dve, S["p_turned"], t)
            dve.tensor_tensor(prob[:, :].rearrange("p (a n) -> p a n", n=N), z,
                              mx[:, :].unsqueeze(2).to_broadcast([P, H, N]), ALU.subtract).then_inc(S["shifted"], 1)

        def low_p(t):
            dve.wait_ge(S["pT_h"], at(t + 1))
            dve.tensor_tensor(pTl[:, :, :], flat(bB).rearrange("p (a n) -> p a n", a=HP), pTh[:, :, :], ALU.subtract)\
                .then_inc(S["pT_l"], 1)

        def normalise(t):
            w = 2 * HD + 1
            dve.wait_ge(S["pv_mm"], at(t + 1))
            acc = bB[:, 0:2, 0:HP * w].rearrange("p b (a n) -> p b a n", n=w)
            dve.reciprocal(rsum[:, :, :], acc[:, :, :, 2 * HD]).then_inc(S["recip"], 1)
            dve.wait_ge(S["recip"], at(t + 1))
            for h in range(2):
                src = slice(h * N, (h + 1) * N)
                for b in range(2):
                    dst = os_[b * N:(b + 1) * N, 0:D].rearrange("p (a h d) -> p a h d", a=HP, h=2)[:, :, h, :]
                    i = dve.tensor_tensor(dst, acc[src, b, :, h * HD:(h + 1) * HD],
                                          rsum[src, b, :].unsqueeze(2).to_broadcast([N, HP, HD]), ALU.mult)
            i.then_inc(S["onormed"], 1)
            dve.wait_ge(S["onormed"], at(t + 1))
            dve.tensor_copy(os_[:, D:D + 2 * TAIL].rearrange("p (a n) -> p a n", a=2),
                            os_[:, E0:D].unsqueeze(1).to_broadcast([P, 2, TAIL])).then_inc(S["ospread"], 1)

        def add_attention(s, l, j):
            t = t_of(s, j)
            x = X[:, bass.ds(at(col(s, l, j)), D)]
            dve.wait_ge(S["proj_mm"], at(t + 1))
            dve.tensor_tensor(tmp[:, :], bB[:, 2, 0:D], gate1[:, :], ALU.mult).then_inc(S["gated"], 1)
            dve.wait_ge(S["gated"], at(t + 1))
            dve.tensor_tensor(x, x, tmp[:, :], ALU.add).then_inc(S["resid"], 1)

        def add_mlp(s, l, j):
            u = t_of(s, j) - 2
            x = X[:, bass.ds(at(col(s, l, j - 2)), D)]
            dve.wait_ge(S["out_mm"], at(u + 1))
            previous(dve, S["resid2"], u)
            dve.tensor_tensor(tmp2[:, :], bM[:, j, 0:D], gate2[:, j, :], ALU.mult).then_inc(S["gated2"], 1)
            dve.wait_ge(S["gated2"], at(u + 1))
            dve.tensor_tensor(x, x, tmp2[:, :], ALU.add).then_inc(S["resid2"], 1)

        def step(s, back, front, mlp):
            for j in range(2):
                t, f = t_of(s, j), front[j]
                if back is not None:
                    if f is not None:
                        moments_one(s, f, j + 1)
                    softmax(t)
                    if f is not None:
                        norm_one(s, f, j + 1)
                        low(yT, turned(bF), S["yTl"], S["yTh"], t + 2)
                    low_p(t)
                    if not isinstance(s, Count) and t == TILES - 1:
                        weights_qkv(1)
                    if f == 1:
                        head_norm(t + 1)
                    if f is not None:
                        split_v(t + 1, (j + 1) % 2)
                    if f == 0:
                        split_qk(t + 1, f, (j + 1) % 2)
                    normalise(t)
                    if f == 1:
                        head_norm_end(t + 1)
                    low(oT, turned(bB), S["oT_l"], S["oT_h"], t + 1)
                    if f == 1:
                        split_qk(t + 1, f, (j + 1) % 2)
                    if f == 0:
                        lay_q(t + 1)
                    add_attention(s, back, j)
                    settle(dve, S["silu_a"])
                    dve.wait_ge(S["resid"], at(t + 1))
                    moments(s, back, j, 1, norm2)
                    if f == 1:
                        lay_q(t + 1)
                    previous(dve, S["y2_turned"], t)
                    norm(s, back, j, 1, norm2)
                    low(y2T[:, :, j * P:(j + 1) * P], turned(bB), S["y2T_l"], S["y2T_h"], t + 1)
                if mlp is not None and j:
                    add_mlp(s, mlp, 0)
                    add_mlp(s, mlp, 1)

        def wanted(l):
            cols = [(2 * D, (j - TILES * l) * D) for j in (-2, -1, 0, 1, 2)]
            return [(2, -2), (2, -1), (2, 0), (2, 1), (2, 2), (2, 3)] + [(2, n - TILES) for n in (1, 2, 3)] * l + cols

        def between(s):
            if s == 0:
                dve.wait_ge(S["p_turned"], 2)
                modulation(1)
                low_bias(1)
            elif s == PAIRS - 1:
                weights_out(1)
            elif s == PAIRS:
                weights_mlp(1)

        dve.memset(half[:, :], -0.5)
        dve.memset(onesf[:, :], 1.0)
        dve.memset(ones[:, :].bitcast(F32), 1.0)
        for t_ in (ys[0], ys[1], os_):
            dve.memset(t_[:, D + 2 * TAIL:3 * P], 1.0)
        for v in v1:
            i = dve.memset(v[:, :, 2 * HD:2 * HD + 1], 1.0)
        i.then_inc(S["consts"], 1)
        dve.memset(qks[:, :, :, 3 * HD:SLOT].bitcast(F32), 0.0)
        dve.memset(qT[0:64, :, :, 1, :].bitcast(F32), 0.0)
        dve.memset(qT[64:128, :, :, 0, :].bitcast(F32), 0.0).then_inc(S["pads"], 1)
        dve.wait_ge(S["silu_a"], 1)
        dve.tensor_scalar(c1[:, :], c1[:, :], 1.0, None, ALU.add).then_inc(S["silu_b"], 1)
        dve.wait_ge(S["silu_b"], 1)
        dve.reciprocal(c1[:, :], c1[:, :]).then_inc(S["silu_c"], 1)
        dve.wait_ge(S["silu_c"], 1)
        dve.tensor_tensor(c0[:, :], c0[:, :], c1[:, :], ALU.mult).then_inc(S["silu_d"], 1)
        dve.wait_ge(S["c_turned"], 1)
        for k in range(3):
            i = dve.tensor_copy(cT[:, k, :].rearrange("p (r n) -> p r n", r=3),
                                bB[0:96, 2, k * 32:(k + 1) * 32].unsqueeze(1).to_broadcast([96, 3, 32]))
        i.then_inc(S["c_copied"], 1)
        low_bias(0)
        modulation(0)
        moments_one(0, 0, 0)
        norm_one(0, 0, 0)
        weights_qkv(0)
        weights_out(0)
        low(yT, turned(bF), S["yTl"], S["yTh"], 1)
        split_v(0, 0)
        split_qk(0, 0, 0)
        lay_q(0)
        weights_mlp(0)
        steps(dve, step, wanted, between)


_OUT = ((B, N, D), "float32")


def kernel(**inputs):
    import numpy as _np
    import concourse.bacc as _bacc
    from concourse import mybir as _mybir
    from concourse.bass_utils import run_bass_kernel_spmd as _run

    nc = _bacc.Bacc("TRN2", target_bir_lowering=False, num_devices=1)
    arrays, io = {}, {}
    for name, value in inputs.items():
        a = _np.ascontiguousarray(value)
        arrays[f"in_{name}_dram"] = a
        io[name] = nc.dram_tensor(f"in_{name}_dram", a.shape, _mybir.dt.from_np(a.dtype), kind="ExternalInput").ap()
    shape, dtype = _OUT
    out = nc.dram_tensor("out_0_dram", shape, _mybir.dt.from_np(_np.dtype(dtype)), kind="ExternalOutput").ap()
    build(nc, io, out)
    r = _run(nc, [arrays], core_ids=[0])
    return r.results[0]["out_0_dram"]
```

```python
from contextlib import ExitStack

import concourse.bass as bass
from concourse import mybir

F32 = mybir.dt.float32
F32R = mybir.dt.float32r
BF16 = mybir.dt.bfloat16
FP16 = mybir.dt.float16
ALU = mybir.AluOpType
ACT = mybir.ActivationFunctionType
AX = mybir.AxisListType

P = 128
B, N, D = 32, 64, 288
H, HD = 16, 18
HP = H // 2
FF = 4 * D
TILES = B * N // P
PAIRS = TILES // 2
EPS = 1e-6
SCALE = float(HD) ** -0.5
A, BB, E, AL, BL = range(5)
E0 = 2 * P
TAIL = D - E0
SLOT = 64
MC = FF // P
SHIFT1, SCALE1, GATE1, SHIFT2, SCALE2, GATE2 = range(6)
PASSES = [(A, A), (A, AL), (AL, A), (BB, BB), (BB, BL), (BL, BB), (E, E)]


class Count:

    def __init__(self, registers, mult=1, add=0):
        self.registers, self.mult, self.add = registers, mult, add

    def __add__(self, n):
        return Count(self.registers, self.mult, self.add + n)

    def __sub__(self, n):
        return self + (-n)

    def __mul__(self, n):
        return Count(self.registers, self.mult * n, self.add * n)

    __radd__, __rmul__ = __add__, __mul__


def at(n):
    return n.registers[n.mult, n.add] if isinstance(n, Count) else n


def counts(engine, s, wanted):
    registers = {(m, a): s * m + a for m, a in wanted}
    for value in registers.values():
        engine.compute_val(value)
    return Count(registers)


def previous(engine, sem, value):
    if isinstance(value, Count) or value > 0:
        engine.wait_ge(sem, at(value))


def settle(engine, sem):
    engine.wait_ge(sem, 1)


def build(nc, io, out):
    ctx = ExitStack()
    with ctx:
        program(nc, ctx, io, out)


def program(nc, ctx, io, out):
    def sb(name, shape, dt=F32):
        return ctx.enter_context(nc.sbuf_tensor(name, shape, dt))

    sems = {}

    def sem(name):
        if name not in sems:
            sems[name] = ctx.enter_context(nc.semaphore(name))
        return sems[name]

    X = sb("X", [P, TILES * D])
    Wqkv = sb("Wqkv", [P, 5, 3 * D], F32R)
    Wout = sb("Wout", [P, 5, D], F32R)
    W1 = sb("W1", [P, 5, FF], F32R)
    W2h = sb("W2h", [P, MC, D], F32R)
    W2l = sb("W2l", [P, MC, D], F32R)
    B2 = sb("B2", [2, D], F32R)
    rawA = sb("rawA", [P, 3, FF])
    rawC = sb("rawC", [P, MC, D])
    raw2 = sb("raw2", [2, D])
    bias = sb("bias", [32, 81])
    biasH = sb("biasH", [32, 81], F32R)
    biasL = sb("biasL", [32, 81])
    mods = [sb(f"mods{l}", [96, 6 * D], BF16) for l in range(2)]
    sel = sb("sel", [96, TILES * P], BF16)
    ident = sb("ident", [P, P])
    ones = sb("ones", [2, P], F32R)
    onesf = sb("onesf", [1, 96])
    half = sb("half", [P, 2 * 2 * H])
    spare = sb("spare", [P, 1])
    gq = sb("gq", [P, HD])
    gk = sb("gk", [P, HD])
    gg = sb("gg", [P, HD])
    ys = [sb(f"ys{j}", [P, 3 * P]) for j in range(2)]
    st = [sb(f"st{j}", [P, 6]) for j in range(2)]
    mv = [sb(f"mv{j}", [P, 2]) for j in range(2)]
    ve = [sb(f"ve{j}", [P, 1]) for j in range(2)]
    rs = [sb(f"rs{j}", [P, 1]) for j in range(2)]
    yT = sb("yT", [P, 5, P], F32R)
    qks = sb("qks", [P, 2, H, SLOT], F32R)
    qT = sb("qT", [P, HP, 2, 2, N], F32R)
    kT = sb("kT", [P, HP * P], F32R)
    prob = sb("prob", [P, H * N])
    pTh = sb("pTh", [P, HP, P], FP16)
    pTl = sb("pTl", [P, HP, P], FP16)
    v1, v2, v3 = ([sb(f"v{n}{j}", [P, HP, 2 * HD + (n == 1)], BF16) for j in range(2)] for n in (1, 2, 3))
    vr = sb("vr", [P, D])
    mx = sb("mx", [P, H])
    rsum = sb("rsum", [P, 2, HP])
    os_ = sb("os", [P, 3 * P])
    oT = sb("oT", [P, 5, P], F32R)
    gate1 = sb("gate1", [P, D])
    gate2 = sb("gate2", [P, 2, D])
    c0, c1 = gate2[0:32, 0, :], gate2[0:32, 1, :]
    tmp = sb("tmp", [P, D])
    tmp2 = sb("tmp2", [P, D])
    y2T = sb("y2T", [P, 5, 2 * P], F32R)
    gl = sb("gl", [P, 3, 2 * P])
    early = gl[:, :, :].rearrange("p a n -> p (a n)")
    plus = early[0:1, 0:D]
    part = early[0:96, D:D + D // 2].bitcast(BF16)
    cT = early[0:96, 432:720].rearrange("p (k n) -> p k n", k=3)
    mod2 = sb("mod2", [P, 2, D])
    hh = sb("hh", [P, MC, 2 * P], F32R)
    hl = sb("hl", [P, MC, 2 * P], F32R)
    shared = sb("shared", [P, 6 * D])
    adab = shared[0:1, :]
    mask = sb("mask", [96, 2])
    *qks2, sq = (shared[:, 2 * a * D:2 * (a + 1) * D].rearrange("p (a h d) -> p a h d", a=2, h=H) for a in range(3))
    s1 = sb("s1", [P, 2 * H])
    s2 = [sb(f"s2{j}", [P, 2 * H]) for j in range(2)]
    mu = sb("mu", [P, 2 * H])
    rq = [sb(f"rq{j}", [P, 2 * H]) for j in range(2)]

    bF, bB, bM = (ctx.enter_context(nc.psum_tensor(f"bank{c}", [P, n, 512], F32)) for c, n in zip("FBM", (3, 3, 2)))

    def flat(t):
        return t[:, 0:2, :].rearrange("p a n -> p (a n)")

    HALF = HP * P // 2
    halves = lambda a: a.rearrange("p (i n) -> p i n", i=2)
    t_of = lambda s, j: 2 * s + j
    col = lambda s, l, j: (s * 2 + (j - TILES * l)) * D

    S = {n: sem(n) for n in """
        x_in ada_in raw_qkv_in raw_w1_in raw_w2_in bias_in c_in g_in ada_free bias_lo_in
        zeroed sel_zero sel_made ident_zero ident_made consts pads silu_a silu_b silu_c silu_d c_turned c_copied mods_mm
        mods_1 mods_rest mods_2 mods_done bias_h bias_l raw2_h
        wqkv_h wqkv_l wout_h wout_l w1_h w1_l w2_h w2_l
        bc1 y_turned qk_mm v_mm q_turned ka_turned k_turned scores0 scores1 p_turned0 p_turned1 pv_mm o_turned proj_mm bc2 y2_turned out_mm
        gate1_out yTh bcg1 bcg2 mod2_out qk_h v_h q_lay ka_lay k_lay exps0 exps1 pT_h0 pT_h1 oT_h y2T_h gate2_out qk_sq
        stats aggr scaled normed spread yTl qk_l v_r v_l q_lay2 maxed0 maxed1 shifted0 shifted1 pT_l0 pT_l1 recip onormed ospread oT_l
        gated resid stats2 aggr2 scaled2 normed2 spread2 y2T_l gated2 resid2 qk_sum qk_mean qk_cent qk_var qk_unit
        eps1 rstd1 eps2 rstd2 v_m qk_eps qk_rstd qk_g g_made stored
    """.split()}
    h_mm = [sem(f"h_mm{c}") for c in range(MC)]
    gelu = [sem(f"gelu{c}") for c in range(MC)]
    h_hi = [sem(f"h_hi{c}") for c in range(MC)]
    h_lo = [sem(f"h_lo{c}") for c in range(MC)]

    W = {"qkv": ["L0_cond_qkv_w", "L1_cond_w_qkv"], "out": ["L0_cond_out_w", "L1_cond_w_proj"],
         "w1": ["L0_cond_w1", "L1_cond_w1"], "w2": ["L0_cond_w2", "L1_cond_w2"],
         "ada": ["L0_cond_ada_w", "L1_cond_w_mod"]}
    Bi = {"qkv": ["L0_cond_qkv_b", "L1_cond_b_qkv"], "out": ["L0_cond_out_b", "L1_cond_b_proj"],
          "w1": ["L0_cond_b1", "L1_cond_b1"], "w2": ["L0_cond_b2", "L1_cond_b2"],
          "ada": ["L0_cond_ada_b", "L1_cond_b_mod"]}
    x_rows = io["x"].rearrange("b n d -> (b n) d")
    out_rows = out.rearrange("b n d -> (b n) d")
    LAST = 2 * PAIRS
    BIAS = {"qkv": (0, 27, 0, 3 * D), "out": (27, 36, 3 * D, FF), "w1": (36, 72, 0, FF), "w2": (72, 81, 0, D)}

    ORDER = (SCALE1, SHIFT1, GATE1, SHIFT2, SCALE2, GATE2)

    def steps(engine, slots, last, wanted, before=lambda s: None):
        def step(s, back, layout, entry, mlp):
            slots[2 * back](s, back, layout, entry, mlp)
            slots[3 if back or layout[1] == 1 else 1](s, back, layout, entry, mlp)

        step(0, 0, (0, 0), 0, None)
        before(1)
        step(1, 0, (0, 0), 0, 0)
        with engine.Fori(2, PAIRS - 1) as s:
            step(counts(engine, s, wanted(0)), 0, (0, 0), 0, 0)
        before(PAIRS - 1)
        step(PAIRS - 1, 0, (0, 1), 1, 0)
        before(PAIRS)
        step(PAIRS, 1, (1, 1), 1, 0)
        before(PAIRS + 1)
        step(PAIRS + 1, 1, (1, 1), 1, 1)
        with engine.Fori(PAIRS + 2, LAST - 1) as s:
            step(counts(engine, s, wanted(1)), 1, (1, 1), 1, 1)
        step(LAST - 1, 1, (1, None), None, 1)
        last(LAST)

    def ada_row(l, k):
        if l == 0 and k < 2:
            return X[0:96, (4 + 6 * k) * D:(10 + 6 * k) * D]
        if k == 2:
            return rawC[0:96, 0:6, :].rearrange("p a n -> p (a n)")
        return rawA[0:96, :, :].rearrange("p a n -> p (a n)")[:, k * 6 * D:(k + 1) * 6 * D]

    block = ctx.enter_context(nc.Block())

    @block.sync
    def _(sp):
        def split_rows(name, l, lo, hi):
            w = io[W[name][l]]
            dmas = [(rawA[:, 0, lo:hi], w[0:P, :]), (rawA[:, 1, lo:hi], w[P:E0, :])]
            return dmas + [(rawA[32 * r:32 * r + 32, 2, lo:hi], w[E0:D, :]) for r in range(3)]

        def load_ada(l):
            w = io[W["ada"][l]].rearrange("(k p) n -> p k n", p=96)
            sp.dma_start(adab[:, :], io[Bi["ada"][l]].rearrange("(a n) -> a n", a=1)).then_inc(S["ada_in"], 16)
            for k in range(3):
                sp.dma_start(ada_row(l, k), w[:, k, :]).then_inc(S["ada_in"], 16)

        def load_qkv_out(l):
            for name in ("qkv", "out"):
                lo, hi = BIAS[name][2:]
                for dst, src in split_rows(name, l, lo, hi):
                    sp.dma_start(dst, src).then_inc(S["raw_qkv_in"], 16)
                sp.dma_start(rawA[96:97, 2, lo:hi], io[Bi[name][l]].rearrange("(a n) -> a n", a=1))\
                    .then_inc(S["raw_qkv_in"], 16)
                sp.dma_start(rawA[97:98, 2, lo:hi], biasL[:, BIAS[name][0]:BIAS[name][1]])\
                    .then_inc(S["raw_qkv_in"], 16)

        def load_w1(l):
            for dst, src in split_rows("w1", l, 0, FF):
                sp.dma_start(dst, src).then_inc(S["raw_w1_in"], 16)
            sp.dma_start(rawA[96:97, 2, :], io[Bi["w1"][l]].rearrange("(a n) -> a n", a=1)).then_inc(S["raw_w1_in"], 16)
            sp.dma_start(rawA[97:98, 2, :], biasL[:, BIAS["w1"][0]:BIAS["w1"][1]]).then_inc(S["raw_w1_in"], 16)

        def load_w2(l):
            sp.dma_start(rawC[:, :, :], io[W["w2"][l]].rearrange("(c p) n -> p c n", p=P)).then_inc(S["raw_w2_in"], 16)
            sp.dma_start(raw2[0:1, :], io[Bi["w2"][l]].rearrange("(a n) -> a n", a=1)).then_inc(S["raw_w2_in"], 16)
            sp.dma_start(raw2[1:2, :], biasL[:, BIAS["w2"][0]:BIAS["w2"][1]]).then_inc(S["raw_w2_in"], 16)

        def load_bias(l):
            for name in ("qkv", "out", "w1", "w2"):
                a, b = BIAS[name][0:2]
                sp.dma_start(bias[:, a:b], io[Bi[name][l]].rearrange("(p n) -> p n", p=32)).then_inc(S["bias_in"], 16)

        def load_x(g):
            sp.dma_start(X[:, g * 4 * D:(g + 1) * 4 * D].rearrange("p (t d) -> p t d", t=4),
                         x_rows[g * 4 * P:(g + 1) * 4 * P, :].rearrange("(t p) d -> p t d", p=P))\
                .then_inc(S["x_in"], 16)

        sp.dma_start(c0[:, :], io["cond_1152"]).then_inc(S["c_in"], 16)
        load_bias(0)
        load_ada(0)
        load_x(0)
        for l in range(2):
            if l:
                for split in ("w1_h", "w1_l", "w2_h", "w2_l"):
                    sp.wait_ge(S[split], 1)
                load_ada(l)
                sp.wait_ge(S["mods_mm"], 12)
            else:
                sp.wait_ge(S["zeroed"], 1)
            sp.wait_ge(S["bias_l"], l + 1)
            load_qkv_out(l)
            if l == 0:
                load_bias(1)
                for dst, name in ((gq, "L1_cond_g_q"), (gk, "L1_cond_g_k")):
                    sp.dma_start(dst[:, :], io[name].rearrange("(a n) -> a n", a=1).to_broadcast([P, HD])).then_inc(S["g_in"], 16)
            else:
                load_w2(l)
            for split in ("wqkv_h", "wqkv_l", "wout_h", "wout_l"):
                sp.wait_ge(S[split], l + 1)
            load_w1(l)
            if l == 0:
                sp.wait_ge(S["mods_mm"], 6)
                load_w2(l)
                for g in range(1, 4):
                    load_x(g)

        def store(s):
            for j in range(2):
                sp.wait_ge(S["resid2"], at(t_of(s, j) - 1))
                sp.dma_start(out_rows[bass.ds(at((s * 2 + (j - TILES - 2)) * P), P), :],
                             X[:, bass.ds(at(col(s, 1, j - 2)), D)]).then_inc(S["stored"], 16)

        with sp.Fori(PAIRS + 1, LAST + 1) as s:
            store(counts(sp, s, [(2, -1), (2, 0)] + [(2 * w, (j - TILES - 2) * w) for w in (D, P) for j in range(2)]))
        sp.wait_ge(S["stored"], 16 * TILES)

    @block.gpsimd
    def _(pool):
        pool.memset(rawA[96:128, 2, :], 0.0).then_inc(S["zeroed"], 1)
        pool.wait_ge(S["zeroed"], 1)
        pool.memset(ident[:, :], 0.0).then_inc(S["ident_zero"], 1)
        pool.wait_ge(S["ident_zero"], 1)
        pool.affine_select(out=ident[:, :], in_=ident[:, :], compare_op=ALU.not_equal, fill=1.0, base=0,
                           pattern=[[-1, P]], channel_multiplier=1).then_inc(S["ident_made"], 1)
        pool.wait_ge(S["ident_made"], 1)
        pool.memset(sel[:, :], 0.0).then_inc(S["sel_zero"], 1)
        pool.wait_ge(S["sel_zero"], 1)
        seq = sel[:, :].rearrange("p (m n) -> p m n", n=N)
        for g in range(3):
            pool.affine_select(out=seq, in_=seq, compare_op=ALU.not_equal, fill=1.0, base=-32 * g,
                               pattern=[[-1, B], [0, N]], channel_multiplier=1).then_inc(S["sel_made"], 1)
            pool.wait_ge(S["sel_made"], g + 1)
        pool.wait_ge(S["g_in"], 32)
        pool.tensor_tensor(gg[:, :], gq[:, :], gk[:, :], ALU.mult).then_inc(S["g_made"], 1)

        def row_scale(t, n, eps_sem, out_sem, var_sem):
            settle(pool, S["consts"])
            pool.wait_ge(var_sem, at(t + 1))
            pool.tensor_scalar(ve[n][:, :], mv[n][:, 1:2], EPS, None, ALU.add).then_inc(eps_sem, 1)
            pool.wait_ge(eps_sem, at(t + 1))
            pool.tensor_tensor(rs[n][:, :], ve[n][:, :], half[:, 0:1], ALU.pow).then_inc(out_sem, 1)

        def head_scale(t, p):
            settle(pool, S["consts"])
            pool.wait_ge(S["qk_var"], at(t + 1))
            pool.tensor_scalar(s2[p][:, :], s2[p][:, :], 1.0 / HD, EPS, ALU.mult, ALU.add).then_inc(S["qk_eps"], 1)
            pool.wait_ge(S["qk_eps"], at(t + 1))
            pool.tensor_tensor(rq[p][:, :], s2[p][:, :], half[:, 0:2 * H], ALU.pow).then_inc(S["qk_rstd"], 1)

        def value_mid(t, p):
            settle(pool, S["consts"])
            pool.wait_ge(S["v_r"], at(t + 1))
            previous(pool, S["pv_mm"], t - 1)
            pool.tensor_scalar(v2[p][:, :, :], vr[:, :].rearrange("p (a n) -> p a n", a=HP), 1.0, 0.0,
                               ALU.mult, ALU.add).then_inc(S["v_m"], 1)

        def hidden(s, c):
            settle(pool, S["consts"])
            pool.wait_ge(gelu[c], at(s))
            previous(pool, S["out_mm"], t_of(s, -2))
            pool.tensor_scalar(hh[:, c, :], gl[:, c % 3, :], 1.0, 0.0, ALU.mult, ALU.add).then_inc(h_hi[c], 1)
            pool.wait_ge(h_hi[c], at(s))
            pool.tensor_tensor(hl[:, c, :], gl[:, c % 3, :], hh[:, c, :].bitcast(F32), ALU.subtract)\
                .then_inc(h_lo[c], 1)

        def slot_1a(s, back, layout, entry, mlp):
            t = t_of(s, 0)
            row_scale(t + 2, 0, S["eps1"], S["rstd1"], S["aggr"])
            if mlp is not None:
                hidden(s, 0)
                hidden(s, 3)
                hidden(s, 1)
                hidden(s, 2)
                hidden(s, 5)
                hidden(s, 4)
            row_scale(t, 1, S["eps2"], S["rstd2"], S["aggr2"])
            value_mid(t + 2, 0)
            if mlp is not None:
                hidden(s, 7)
                hidden(s, 6)
                hidden(s, 8)
            if entry == 1:
                head_scale(t + 2 - TILES, 0)

        def slot_1b(s, back, layout, entry, mlp):
            t = t_of(s, 0)
            row_scale(t + 3, 0, S["eps1"], S["rstd1"], S["aggr"])
            row_scale(t + 1, 1, S["eps2"], S["rstd2"], S["aggr2"])
            value_mid(t + 3, 1)

        def slot_2a(s, back, layout, entry, mlp):
            t = t_of(s, 0)
            if entry is not None:
                row_scale(t + 2, 0, S["eps1"], S["rstd1"], S["aggr"])
            hidden(s, 1)
            hidden(s, 0)
            hidden(s, 2)
            hidden(s, 4)
            hidden(s, 3)
            hidden(s, 5)
            hidden(s, 6)
            if entry is not None:
                value_mid(t + 2, 0)
            row_scale(t, 1, S["eps2"], S["rstd2"], S["aggr2"])
            hidden(s, 7)
            if entry is not None:
                head_scale(t + 2 - TILES, 0)
            hidden(s, 8)

        def slot_2b(s, back, layout, entry, mlp):
            t = t_of(s, 0)
            if entry is not None:
                row_scale(t + 3, 0, S["eps1"], S["rstd1"], S["aggr"])
                value_mid(t + 3, 1)
            row_scale(t + 1, 1, S["eps2"], S["rstd2"], S["aggr2"])
            if entry is not None:
                head_scale(t + 3 - TILES, 1)

        def last(s):
            for c in range(MC):
                hidden(s, c)

        def wanted(l):
            return [(1, 0), (2, -2), (2, 0), (2, 1), (2, 2), (2, 3), (2, 4)] + [(2, n - TILES) for n in (3, 4)] * l

        pool.wait_ge(S["consts"], 1)
        row_scale(0, 0, S["eps1"], S["rstd1"], S["aggr"])
        value_mid(0, 0)
        row_scale(1, 0, S["eps1"], S["rstd1"], S["aggr"])
        value_mid(1, 1)
        steps(pool, (slot_1a, slot_1b, slot_2a, slot_2b), last, wanted)

    @block.scalar
    def _(act):
        def cast(dst, src, sem=None):
            i = act.activation(dst, src, ACT.Copy)
            return i.then_inc(sem, 1) if sem is not None else i

        def weights_qkv(l):
            act.wait_ge(S["raw_qkv_in"], 16 * 14 * (l + 1))
            previous(act, S["v_mm"], TILES * l)
            for k in range(3):
                i = cast(Wqkv[:, k, :], rawA[:, k, 0:3 * D])
            i.then_inc(S["wqkv_h"], 1)

        def weights_out(l):
            previous(act, S["proj_mm"], TILES * l)
            cast(Wout[:, 0:3, :], rawA[:, :, 3 * D:FF], S["wout_h"])

        def weights_w1(l):
            act.wait_ge(S["raw_w1_in"], 16 * 7 * (l + 1))
            previous(act, h_mm[MC - 1], PAIRS * l)
            for k in range(3):
                i = cast(W1[:, k, :], rawA[:, k, :])
            i.then_inc(S["w1_h"], 1)

        def weights_w2(l):
            act.wait_ge(S["raw_w2_in"], 16 * 3 * (l + 1))
            previous(act, S["out_mm"], TILES * l)
            cast(B2[:, :], raw2[:, :])
            cast(W2h[:, :, :], rawC[:, :, :], S["w2_h"])

        def modulation(l, m):
            n = 6 * l + m + 1
            act.wait_ge(S["mods_mm"], n)
            previous(act, S["mods_done"], n - 1)
            cast(part[:, :], bM[0:96, m % 2, 0:D], S["mods_1"])
            act.wait_ge(S["mods_rest"], n)
            cast(part[:, :], tmp2[0:96, :], S["mods_2"])

        def high_bias(l):
            act.wait_ge(S["bias_in"], 64 * (l + 1))
            previous(act, S["bias_l"], l)
            cast(biasH[:, :], bias[:, :], S["bias_h"])

        def gate_one(t):
            act.wait_ge(S["bcg1"], at(t + 1))
            previous(act, S["gated"], t)
            cast(gate1[:, :], bB[:, 2, 0:D], S["gate1_out"])

        def turned_y(t):
            act.wait_ge(S["y_turned"], at(t + 1))
            previous(act, S["v_mm"], t)
            cast(yT[:, 0:3, :], bF[:, 2, 0:3 * P].rearrange("p (k n) -> p k n", k=3), S["yTh"])

        def split_v(t, p):
            act.wait_ge(S["v_mm"], at(t + 1))
            previous(act, S["pv_mm"], t - 1)
            cast(v1[p][:, :, 0:2 * HD], bF[:, 2, 0:D].rearrange("p (a n) -> p a n", a=HP), S["v_h"])

        def squares(t, p):
            act.wait_ge(S["qk_cent"], at(t + 1 - TILES))
            act.activation(sq[:, :, :, :], qks2[p][:, :, :, :], ACT.Square).then_inc(S["qk_sq"], 1)

        def split_qk(t, l, p):
            previous(act, S["k_turned"], t)
            if l:
                act.wait_ge(S["qk_g"], at(t + 1 - TILES))
                q, k = qks2[p][:, 0, :, :], qks2[p][:, 1, :, :]
            else:
                act.wait_ge(S["qk_mm"], at(t + 1))
                q, k = (bF[:, a, 0:D].rearrange("p (h d) -> p h d", h=H) for a in range(2))
            cast(qks[:, 0, :, 0:HD], q)
            cast(qks[:, 0, :, 2 * HD:3 * HD], q)
            cast(qks[:, 1, :, 0:HD], k)
            cast(qks[:, 1, :, HD:2 * HD], k, S["qk_h"])

        def lay_q(t):
            act.wait_ge(S["q_turned"], at(t + 1))
            previous(act, S["scores1"], t)
            cast(qT[0:64, :, :, 0, :], flat(bF)[0:64, :].rearrange("p (a b q) -> p a b q", a=HP, b=2), S["q_lay"])

        def lay_ka(t):
            act.wait_ge(S["ka_turned"], at(t + 1))
            previous(act, S["scores1"], t)
            cast(kT[:, 0:HALF], bF[:, 2, :], S["ka_lay"])

        def lay_kb(t):
            act.wait_ge(S["k_turned"], at(t + 1))
            cast(kT[:, HALF:2 * HALF], bF[:, 0, :], S["k_lay"])

        def exp(t, i):
            act.wait_ge(S[f"shifted{i}"], at(t + 1))
            act.activation(halves(prob[:, :])[:, i, :], halves(prob[:, :])[:, i, :], ACT.Exp, scale=SCALE)\
                .then_inc(S[f"exps{i}"], 1)

        def load_exp():
            act.wait_ge(S["consts"], 1)
            act.activation(spare[:, :], half[:, 0:1], ACT.Exp)

        def turned_p(t, i):
            act.wait_ge(S[f"p_turned{i}"], at(t + 1))
            previous(act, S["pv_mm"], t)
            cast(pTh[:, 4 * i:4 * i + 4, :], bB[:, i, :].rearrange("p (a n) -> p a n", a=HP // 2), S[f"pT_h{i}"])

        def turned_o(t):
            act.wait_ge(S["o_turned"], at(t + 1))
            previous(act, S["proj_mm"], t)
            cast(oT[:, 0:3, :], bB[:, 2, 0:3 * P].rearrange("p (k n) -> p k n", k=3), S["oT_h"])

        def turned_y2(s, j):
            t = t_of(s, j)
            act.wait_ge(S["y2_turned"], at(t + 1))
            previous(act, h_mm[MC - 1], s)
            cast(y2T[:, 0:3, j * P:(j + 1) * P], bB[:, 2, 0:3 * P].rearrange("p (k n) -> p k n", k=3), S["y2T_h"])

        def modulation_two(t):
            act.wait_ge(S["bc2"], at(t + 1))
            previous(act, S["normed2"], t)
            cast(mod2[:, :, :], bF[:, 0:2, 0:D], S["mod2_out"])

        def gate_two(s, j):
            act.wait_ge(S["bcg2"], at(t_of(s, j) - 1))
            previous(act, S["gated2"], t_of(s, j) - 3)
            cast(gate2[:, j, :], bB[:, 2, 0:D], S["gate2_out"])

        def hidden(s, c):
            act.wait_ge(h_mm[c], at(s))
            if c >= 3:
                act.wait_ge(h_lo[c - 3], at(s))
            else:
                previous(act, h_lo[MC - 3 + c], s - 1)
            act.activation(gl[:, c % 3, :], bM[:, c % 2, 0:2 * P], ACT.Gelu_apprx_tanh).then_inc(gelu[c], 1)

        def slot_1a(s, back, layout, entry, mlp):
            t = t_of(s, 0)
            aside(s, 4)
            gate_one(t)
            turned_p(t, 0)
            turned_p(t, 1)
            if mlp is not None:
                gate_two(s, 0)
            lay_q(t + 1)
            if mlp is not None:
                hidden(s, 0)
                hidden(s, 1)
            lay_kb(t + 1)
            lay_ka(t + 1)
            modulation_two(t)
            if mlp is not None:
                hidden(s, 3)
            turned_o(t)
            if mlp is not None:
                hidden(s, 2)
            turned_y(t + 2)
            aside(s, 0)
            if mlp is not None:
                hidden(s, 4)
                hidden(s, 5)
            exp(t + 1, 0)
            if mlp is not None:
                load_exp()
            exp(t + 1, 1)
            if mlp is not None:
                hidden(s, 6)
            split_v(t + 2, 0)
            if entry == 0:
                split_qk(t + 2, 0, 0)
            aside(s, 1)
            if mlp is not None:
                hidden(s, 8)
            turned_y2(s, 0)
            if mlp is not None:
                hidden(s, 7)
            if entry == 1:
                squares(t + 2, 0)

        def slot_1b(s, back, layout, entry, mlp):
            t = t_of(s, 0)
            turned_p(t + 1, 0)
            gate_one(t + 1)
            turned_p(t + 1, 1)
            if mlp is not None:
                gate_two(s, 1)
            lay_q(t + 2)
            lay_kb(t + 2)
            modulation_two(t + 1)
            lay_ka(t + 2)
            turned_o(t + 1)
            aside(s, 2)
            turned_y(t + 3)
            exp(t + 2, 0)
            split_v(t + 3, 1)
            exp(t + 2, 1)
            split_qk(t + 3, 0, 1)
            aside(s, 3)
            turned_y2(s, 1)

        def slot_2a(s, back, layout, entry, mlp):
            t = t_of(s, 0)
            turned_p(t, 0)
            turned_p(t, 1)
            gate_one(t)
            modulation_two(t)
            gate_two(s, 0)
            hidden(s, 0)
            hidden(s, 1)
            hidden(s, 2)
            if entry is not None:
                turned_y(t + 2)
            hidden(s, 3)
            split_qk(t + 1, 1, 1)
            hidden(s, 4)
            hidden(s, 5)
            turned_o(t)
            if entry is not None:
                split_v(t + 2, 0)
            aside(s, 6)
            if entry is not None:
                squares(t + 2, 0)
            hidden(s, 6)
            lay_q(t + 1)
            hidden(s, 7)
            lay_ka(t + 1)
            lay_kb(t + 1)
            hidden(s, 8)
            load_exp()
            turned_y2(s, 0)
            exp(t + 1, 0)
            exp(t + 1, 1)

        def slot_2b(s, back, layout, entry, mlp):
            t = t_of(s, 0)
            turned_p(t + 1, 0)
            gate_one(t + 1)
            modulation_two(t + 1)
            gate_two(s, 1)
            turned_p(t + 1, 1)
            if entry is not None:
                turned_y(t + 3)
            if layout[1] is not None:
                split_qk(t + 2, 1, 0)
            turned_o(t + 1)
            if entry is not None:
                split_v(t + 3, 1)
            if layout[1] is not None:
                lay_q(t + 2)
            if entry is not None:
                squares(t + 3, 1)
            aside(s, 5)
            if layout[1] is not None:
                lay_ka(t + 2)
                lay_kb(t + 2)
            turned_y2(s, 1)
            if layout[1] is not None:
                exp(t + 2, 0)
                exp(t + 2, 1)

        def last(s):
            gate_two(s, 0)
            for c in range(MC):
                hidden(s, c)
            gate_two(s, 1)

        def wanted(l):
            return [(1, 0), (1, -1), (2, -3), (2, -2), (2, -1), (2, 0), (2, 1), (2, 2), (2, 3), (2, 4)] + \
                [(2, n - TILES) for n in (1, 2, 3, 4)] * l

        def aside(s, place):
            if isinstance(s, Count) or s != (0, 0, 0, 0, PAIRS - 1, PAIRS, PAIRS + 1)[place]:
                return
            if place == 4:
                weights_qkv(1)
            elif place == 5:
                weights_w1(1)
            elif place == 6:
                weights_w2(1)
            elif place == 0:
                weights_w1(0)
            elif place == 1:
                weights_w2(0)
                high_bias(1)
            else:
                for m in range(3 * (place - 2), 3 * (place - 1)):
                    modulation(1, m)

        def before(s):
            if s == 1:
                act.wait_ge(S["mods_done"], 12)
            elif s == PAIRS:
                weights_out(1)

        act.wait_ge(S["c_in"], 16)
        act.activation(c1[:, :], c0[:, :], ACT.Exp, scale=-1.0).then_inc(S["silu_a"], 1)
        high_bias(0)
        modulation(0, 0)
        modulation(0, 1)
        weights_qkv(0)
        modulation(0, 2)
        turned_y(0)
        weights_out(0)
        modulation(0, 3)
        split_v(0, 0)
        split_qk(0, 0, 0)
        modulation(0, 4)
        lay_q(0)
        lay_ka(0)
        lay_kb(0)
        modulation(0, 5)
        turned_y(1)
        exp(0, 0)
        exp(0, 1)
        split_v(1, 1)
        split_qk(1, 0, 1)
        steps(act, (slot_1a, slot_1b, slot_2a, slot_2b), last, wanted, before)

    @block.tensor
    def _(pe):
        def product(outs, stationary, moving, sem):
            for n, (a, b) in enumerate(PASSES):
                for o, cols in outs:
                    i = pe.matmul(o, stationary[:, a, :], moving[:, b, cols], start=(n == 0),
                                  stop=(n == len(PASSES) - 1), skip_group_check=True)
            i.then_inc(sem, 1)

        def turn_three(dst, src, sem):
            for k in range(3):
                i = pe.transpose(dst[:, k * P:(k + 1) * P], src[:, k * P:(k + 1) * P], ident[:, :])
            i.then_inc(sem, 1)

        def modulation(l, m):
            if m == 0:
                pe.wait_ge(S["ada_in"], 64 * (l + 1))
            previous(pe, S["mods_rest"], 6 * l + m - 1)
            b, c = bM[0:96, m % 2, 0:D], ORDER[m] * D
            for k in range(3):
                pe.matmul(b, cT[:, k, :], ada_row(l, k)[:, c:c + D], start=(k == 0), stop=False)
            if ORDER[m] in (SCALE1, SCALE2):
                pe.matmul(b, onesf[:, :], plus[:, :], start=False, stop=False)
            pe.matmul(b, onesf[:, :], adab[:, c:c + D], start=False, stop=True).then_inc(S["mods_mm"], 1)

        def spread(s, l, j, which, dst):
            tile = bass.ds(at((s * 2 + (j - TILES * l)) * P), P)
            for m, d in zip(which, dst):
                i = pe.matmul(d, sel[:, tile], mods[l][:, m * D:(m + 1) * D], start=True, stop=True)
            return i

        def spread_one(s, l, j, laid):
            t = t_of(s, j)
            for side in ("k_lay", "q_lay", "q_lay2"):
                previous(pe, S[side], t - 1 + laid)
            previous(pe, S["mod2_out"], t - 1)
            spread(s, l, j, (SCALE1, SHIFT1), (bF[:, 0, 0:D], bF[:, 1, 0:D])).then_inc(S["bc1"], 1)

        def spread_gate1(s, l, j):
            t = t_of(s, j)
            previous(pe, S["y2T_l"], t)
            previous(pe, S["y2T_h"], t)
            spread(s, l, j, (GATE1,), (bB[:, 2, 0:D],)).then_inc(S["bcg1"], 1)

        def turn_y(t, laid):
            pe.wait_ge(S["spread"], at(t + 1))
            previous(pe, S["ka_lay"], t - 1 + laid)
            turn_three(bF[:, 2, :], ys[0], S["y_turned"])

        def qk_product(t):
            pe.wait_ge(S["yTh"], at(t + 1))
            pe.wait_ge(S["yTl"], at(t + 1))
            product([(bF[:, m, 0:D], slice(m * D, (m + 1) * D)) for m in range(2)], yT, Wqkv, S["qk_mm"])

        def v_product(t):
            pe.wait_ge(S["yTh"], at(t + 1))
            pe.wait_ge(S["yTl"], at(t + 1))
            product([(bF[:, 2, 0:D], slice(2 * D, 3 * D))], yT, Wqkv, S["v_mm"])

        def turn_q(t, l, entry):
            if entry is not None:
                pe.wait_ge(S["qk_cent"], at(t + 2 - TILES))
            if l:
                pe.wait_ge(S["mod2_out"], at(t))
            pe.wait_ge(S["qk_h"], at(t + 1))
            pe.wait_ge(S["qk_l"], at(t + 1))
            turn_pairs(0, range(HP), flat(bF), S["q_turned"])

        def turn_ka(t, entry):
            pe.wait_ge(S["qk_h"], at(t + 1))
            pe.wait_ge(S["qk_l"], at(t + 1))
            for read in ("v_r", "v_h"):
                pe.wait_ge(S[read], at(t + (1 if entry is None else 2)))
            turn_pairs(1, range(HP // 2), bF[:, 2, :], S["ka_turned"])

        def turn_kb(t):
            pe.wait_ge(S["q_lay"], at(t + 1))
            pe.wait_ge(S["q_lay2"], at(t + 1))
            turn_pairs(1, range(HP // 2, HP), bF[:, 0, :], S["k_turned"])

        def turn_pairs(which, pairs, dst, done):
            src = qks[:, which, :, :].rearrange("p h c -> p (h c)").bitcast(F32)
            for n, a in enumerate(pairs):
                i = pe.transpose(dst[:, n * P:(n + 1) * P], src[:, a * P:(a + 1) * P], ident[:, :])
            i.then_inc(done, 1)

        def scores(t, i):
            for laid in ("q_lay", "q_lay2", "ka_lay", "k_lay"):
                pe.wait_ge(S[laid], at(t + 1))
            previous(pe, S["onormed"], t)
            for a in range(HP // 2):
                pair = i * HP // 2 + a
                for b in range(2):
                    c = (2 * a + b) * N
                    last_ = pe.matmul(bB[:, i, c:c + N], qT[:, pair, b, :, :].rearrange("p h q -> p (h q)"),
                                      kT[:, pair * P + b * N:pair * P + (b + 1) * N], start=True, stop=True)
            last_.then_inc(S[f"scores{i}"], 1)

        def turn_p(t, i):
            pe.wait_ge(S[f"exps{i}"], at(t + 1))
            for a in range(HP // 2):
                last_ = pe.transpose(bB[:, i, a * P:(a + 1) * P], halves(prob[:, :])[:, i, a * P:(a + 1) * P], ident[:, :])
            last_.then_inc(S[f"p_turned{i}"], 1)

        def pv(t, par, i, mlp):
            pe.wait_ge(S["gate1_out"], at(t + 1))
            if mlp is not None:
                pe.wait_ge(S["gate2_out"], at(t - 1))
            pe.wait_ge(S["v_l"], at(t + 1))
            pe.wait_ge(S["v_m"], at(t + 1))
            pe.wait_ge(S[f"pT_h{i}"], at(t + 1))
            pe.wait_ge(S[f"pT_l{i}"], at(t + 1))
            for a in range(i * HP // 2, (i + 1) * HP // 2):
                for n, (p, v) in enumerate(((pTh, v1[par]), (pTh, v2[par]), (pTh, v3[par]), (pTl, v1[par]), (pTl, v2[par]))):
                    for b in range(2):
                        rows = slice(b * N, (b + 1) * N)
                        w = v.shape[2]
                        c = (a if b else a % (HP // 2)) * (2 * HD + 1)
                        last_ = pe.matmul(bB[:, 2 if b else i, c:c + w], p[rows, a, :], v[rows, a, :], start=(n == 0),
                                          stop=(n == 4), skip_group_check=True)
            if i:
                last_.then_inc(S["pv_mm"], 1)

        def turn_o(t):
            pe.wait_ge(S["ospread"], at(t + 1))
            turn_three(bB[:, 2, :], os_, S["o_turned"])

        def project(t):
            pe.wait_ge(S["oT_h"], at(t + 1))
            pe.wait_ge(S["oT_l"], at(t + 1))
            product([(bB[:, 2, 0:D], slice(0, D))], oT, Wout, S["proj_mm"])

        def spread_two(s, l, j, laid):
            for side in ("k_lay", "q_lay", "q_lay2"):
                pe.wait_ge(S[side], at(t_of(s, j) + laid))
            spread(s, l, j, (SCALE2, SHIFT2), (bF[:, 0, 0:D], bF[:, 1, 0:D])).then_inc(S["bc2"], 1)

        def turn_y2(t):
            pe.wait_ge(S["spread2"], at(t + 1))
            turn_three(bB[:, 2, :], ys[1], S["y2_turned"])

        def spread_gate2(s, l, j):
            pe.wait_ge(S["gate1_out"], at(t_of(s, j) + 1))
            spread(s, l, j - 2, (GATE2,), (bB[:, 2, 0:D],)).then_inc(S["bcg2"], 1)

        def hidden(s, c):
            if c == 0:
                pe.wait_ge(S["y2T_h"], at(t_of(s, 0)))
                pe.wait_ge(S["y2T_l"], at(t_of(s, 0)))
            if c < 2:
                previous(pe, S["gated2"], t_of(s, -2) - 1 + c)
            else:
                pe.wait_ge(gelu[c - 2], at(s))
            for n, (a, b) in enumerate(PASSES):
                i = pe.matmul(bM[:, c % 2, 0:2 * P], W1[:, a, c * P:(c + 1) * P], y2T[:, b, :],
                              start=(n == 0), stop=(n == len(PASSES) - 1))
            i.then_inc(h_mm[c], 1)

        def second(s, j, *chunks):
            o = bM[:, j, 0:D]
            for c in chunks:
                if c == 0:
                    pe.wait_ge(gelu[MC - 1 - j], at(s))
                    pe.matmul(o, ones[:, :], B2[:, :], start=True, stop=False)
                pe.wait_ge(h_hi[c], at(s))
                pe.wait_ge(h_lo[c], at(s))
                tile = slice(j * P, (j + 1) * P)
                for hid, w in ((hh, W2h), (hh, W2l), (hl, W2h)):
                    i = pe.matmul(o, hid[:, c, tile], w[:, c, :], start=False,
                                  stop=(c == MC - 1 and w is W2h and hid is hl))
                if c == MC - 1:
                    i.then_inc(S["out_mm"], 1)

        def slot_1a(s, back, layout, entry, mlp):
            t = t_of(s, 0)
            spread_gate1(s, back, 0)
            if mlp is not None:
                hidden(s, 0)
            turn_q(t + 1, 0, None)
            if mlp is not None:
                spread_gate2(s, mlp, 0)
                hidden(s, 1)
            pv(t, 0, 0, mlp)
            turn_kb(t + 1)
            pv(t, 0, 1, mlp)
            turn_ka(t + 1, None)
            if mlp is not None:
                hidden(s, 2)
            spread_two(s, back, 0, 2)
            if mlp is not None:
                hidden(s, 3)
            turn_o(t)
            spread_one(s, entry, 2, 1)
            scores(t + 1, 0)
            if mlp is not None:
                hidden(s, 4)
            scores(t + 1, 1)
            turn_y(t + 2, 1)
            if mlp is not None:
                hidden(s, 5)
            project(t)
            if mlp is not None:
                hidden(s, 6)
            aside(s, 4)
            qk_product(t + 2)
            v_product(t + 2)
            if mlp is not None:
                hidden(s, 7)
            turn_p(t + 1, 0)
            if mlp is not None:
                hidden(s, 8)
            turn_y2(t)
            turn_p(t + 1, 1)

        def slot_1b(s, back, layout, entry, mlp):
            t = t_of(s, 0)
            if mlp is not None:
                second(s, 0, 0)
            turn_q(t + 2, 0, None)
            spread_gate1(s, back, 1)
            if mlp is not None:
                second(s, 1, 0)
                second(s, 0, 1)
                spread_gate2(s, mlp, 1)
                second(s, 1, 1)
                second(s, 0, 2)
            pv(t + 1, 1, 0, mlp)
            turn_kb(t + 2)
            pv(t + 1, 1, 1, mlp)
            spread_two(s, back, 1, 2)
            turn_ka(t + 2, None)
            if mlp is not None:
                second(s, 0, 3)
                second(s, 1, 2)
            spread_one(s, entry, 3, 1)
            if mlp is not None:
                second(s, 0, 4)
            turn_o(t + 1)
            if mlp is not None:
                second(s, 1, 3)
            aside(s, 2)
            scores(t + 2, 0)
            turn_y(t + 3, 1)
            if mlp is not None:
                second(s, 0, 5)
            project(t + 1)
            if mlp is not None:
                second(s, 1, 4)
            scores(t + 2, 1)
            if mlp is not None:
                second(s, 0, 6)
            v_product(t + 3)
            if mlp is not None:
                second(s, 0, 7)
            qk_product(t + 3)
            if mlp is not None:
                second(s, 1, 5)
            aside(s, 3)
            if mlp is not None:
                second(s, 0, 8)
                second(s, 1, 6)
            turn_y2(t + 1)
            if mlp is not None:
                second(s, 1, 7)
            turn_p(t + 2, 0)
            if mlp is not None:
                second(s, 1, 8)
            turn_p(t + 2, 1)

        def slot_2a(s, back, layout, entry, mlp):
            t = t_of(s, 0)
            spread_two(s, back, 0, 1)
            spread_gate1(s, back, 0)
            hidden(s, 0)
            spread_gate2(s, mlp, 0)
            hidden(s, 1)
            if entry is not None:
                spread_one(s, entry, 2, 0)
            pv(t, 0, 0, mlp)
            hidden(s, 2)
            pv(t, 0, 1, mlp)
            hidden(s, 3)
            if entry is not None:
                turn_y(t + 2, 0)
            hidden(s, 4)
            turn_o(t)
            hidden(s, 5)
            if entry is not None:
                qk_product(t + 2)
                v_product(t + 2)
            project(t)
            hidden(s, 6)
            turn_q(t + 1, 1, entry)
            hidden(s, 7)
            turn_ka(t + 1, entry)
            turn_kb(t + 1)
            hidden(s, 8)
            scores(t + 1, 0)
            scores(t + 1, 1)
            turn_y2(t)
            turn_p(t + 1, 0)
            turn_p(t + 1, 1)

        def slot_2b(s, back, layout, entry, mlp):
            t = t_of(s, 0)
            spread_gate1(s, back, 1)
            spread_two(s, back, 1, 1)
            aside(s, 6)
            second(s, 1, 0)
            spread_gate2(s, mlp, 1)
            second(s, 1, 1)
            if entry is not None:
                spread_one(s, entry, 3, 0)
            pv(t + 1, 1, 0, mlp)
            pv(t + 1, 1, 1, mlp)
            second(s, 0, 0)
            if entry is not None:
                turn_y(t + 3, 0)
            second(s, 1, 2)
            second(s, 0, 1)
            second(s, 0, 2)
            turn_o(t + 1)
            if entry is not None:
                qk_product(t + 3)
            second(s, 0, 3)
            if entry is not None:
                v_product(t + 3)
            project(t + 1)
            if layout[1] is not None:
                turn_q(t + 2, 1, entry)
            second(s, 1, 3)
            second(s, 0, 4)
            second(s, 0, 5)
            if layout[1] is not None:
                turn_ka(t + 2, entry)
                turn_kb(t + 2)
            second(s, 1, 4)
            second(s, 1, 5)
            if layout[1] is not None:
                scores(t + 2, 0)
            second(s, 0, 6)
            if layout[1] is not None:
                scores(t + 2, 1)
            turn_y2(t + 1)
            second(s, 0, 7)
            second(s, 1, 6)
            second(s, 1, 7)
            if layout[1] is not None:
                turn_p(t + 2, 0)
            second(s, 0, 8)
            second(s, 1, 8)
            if layout[1] is not None:
                turn_p(t + 2, 1)

        def last(s):
            t = t_of(s, 0)
            pe.wait_ge(S["y2T_h"], t)
            pe.wait_ge(S["y2T_l"], t)
            spread(s, 1, -2, (GATE2,), (bB[:, 2, 0:D],)).then_inc(S["bcg2"], 1)
            for c in range(MC):
                hidden(s, c)
            pe.wait_ge(S["gate2_out"], t - 1)
            spread(s, 1, -1, (GATE2,), (bB[:, 2, 0:D],)).then_inc(S["bcg2"], 1)
            second(s, 0, *range(MC))
            second(s, 1, *range(MC))

        def wanted(l):
            tiles = [(2 * P, (j - TILES * l) * P) for j in (-2, -1, 0, 1, 2, 3)]
            return [(1, 0), (2, -3), (2, -2), (2, -1), (2, 0), (2, 1), (2, 2), (2, 3), (2, 4)] + \
                [(2, n - TILES) for n in (3, 4)] * l + tiles

        def aside(s, place):
            if isinstance(s, Count):
                return
            if place == 4 and s == PAIRS - 1:
                pe.wait_ge(S["wqkv_h"], 2)
                pe.wait_ge(S["wqkv_l"], 2)
            elif place == 6 and s == PAIRS + 1:
                pe.wait_ge(S["w2_h"], 2)
                pe.wait_ge(S["w2_l"], 2)
            elif place < 4 and s == 0:
                for m in range(3 * (place - 2), 3 * (place - 1)):
                    modulation(1, m)

        def before(s):
            if s in (1, PAIRS + 1):
                if s == 1:
                    pe.wait_ge(S["mods_rest"], 12)
                for split in ("w1_h", "w1_l") + ("w2_h", "w2_l") * (s == 1):
                    pe.wait_ge(S[split], s // PAIRS + 1)
            elif s == PAIRS - 1:
                pe.wait_ge(S["mods_done"], 12)
            elif s == PAIRS:
                pe.wait_ge(S["wout_h"], 2)
                pe.wait_ge(S["wout_l"], 2)

        pe.wait_ge(S["ident_made"], 1)
        pe.wait_ge(S["silu_d"], 1)
        for k in range(3):
            i = pe.transpose(bB[0:96, 2, k * 32:(k + 1) * 32], c0[:, k * 96:(k + 1) * 96], ident[0:32, 0:32])
        i.then_inc(S["c_turned"], 1)
        pe.wait_ge(S["c_copied"], 1)
        pe.wait_ge(S["consts"], 1)
        pe.wait_ge(S["sel_made"], 3)
        modulation(0, 0)
        modulation(0, 1)
        modulation(0, 2)
        pe.wait_ge(S["mods_done"], 2)
        spread_one(0, 0, 0, 1)
        modulation(0, 3)
        turn_y(0, 1)
        modulation(0, 4)
        pe.wait_ge(S["wqkv_h"], 1)
        pe.wait_ge(S["wqkv_l"], 1)
        qk_product(0)
        v_product(0)
        modulation(0, 5)
        pe.wait_ge(S["pads"], 1)
        turn_q(0, 0, None)
        turn_ka(0, None)
        turn_kb(0)
        spread_one(0, 0, 1, 1)
        turn_y(1, 1)
        scores(0, 0)
        scores(0, 1)
        qk_product(1)
        turn_p(0, 0)
        turn_p(0, 1)
        v_product(1)
        pe.wait_ge(S["wout_h"], 1)
        pe.wait_ge(S["wout_l"], 1)
        pe.wait_ge(S["mods_done"], 6)
        steps(pe, (slot_1a, slot_1b, slot_2a, slot_2b), last, wanted, before)

    @block.vector
    def _(dve):
        def weights_qkv(l):
            dve.wait_ge(S["wqkv_h"], l + 1)
            dve.tensor_tensor(Wqkv[:, AL:BL + 1, :], rawA[:, 0:2, 0:3 * D], Wqkv[:, A:BB + 1, :].bitcast(F32), ALU.subtract)
            dve.tensor_tensor(Wqkv[64:96, E, :], rawA[64:96, 2, 0:3 * D], Wqkv[64:96, E, :].bitcast(F32), ALU.subtract)\
                .then_inc(S["wqkv_l"], 1)

        def weights_out(l):
            dve.wait_ge(S["wout_h"], l + 1)
            dve.tensor_tensor(Wout[:, AL:BL + 1, :], rawA[:, 0:2, 3 * D:FF], Wout[:, A:BB + 1, :].bitcast(F32), ALU.subtract)
            dve.tensor_tensor(Wout[64:96, E, :], rawA[64:96, 2, 3 * D:FF], Wout[64:96, E, :].bitcast(F32), ALU.subtract)\
                .then_inc(S["wout_l"], 1)

        def weights_w1(l):
            dve.wait_ge(S["w1_h"], l + 1)
            dve.tensor_tensor(W1[:, AL:BL + 1, :], rawA[:, 0:2, :], W1[:, A:BB + 1, :].bitcast(F32), ALU.subtract)
            dve.tensor_tensor(W1[64:96, E, :], rawA[64:96, 2, :], W1[64:96, E, :].bitcast(F32), ALU.subtract)\
                .then_inc(S["w1_l"], 1)

        def weights_w2(l):
            dve.wait_ge(S["w2_h"], l + 1)
            dve.tensor_tensor(W2l[:, :, :], rawC[:, :, :], W2h[:, :, :].bitcast(F32), ALU.subtract).then_inc(S["w2_l"], 1)

        def modulation(l, m):
            n = 6 * l + m + 1
            dve.wait_ge(S["mods_1"], n)
            dve.scalar_tensor_tensor(tmp2[0:96, :], part[:, :], mask[:, 0:1], bM[0:96, m % 2, 0:D], ALU.mult, ALU.add)\
                .then_inc(S["mods_rest"], 1)
            dve.wait_ge(S["mods_2"], n)
            dve.scalar_tensor_tensor(mods[l][:, ORDER[m] * D:(ORDER[m] + 1) * D], part[:, :], mask[:, 1:2],
                                     tmp2[0:96, :], ALU.mult, ALU.add).then_inc(S["mods_done"], 1)

        def low_bias(l):
            dve.wait_ge(S["bias_h"], l + 1)
            if l:
                dve.wait_ge(S["w1_h"], 1)
                dve.wait_ge(S["w2_h"], 1)
            dve.tensor_tensor(biasL[:, :], bias[:, :], biasH[:, :].bitcast(F32), ALU.subtract).then_inc(S["bias_l"], 1)

        def moments(s, l, j, n, sems):
            t = t_of(s, j)
            stats, aggr = sems[0:2]
            previous(dve, sems[5], t)
            dve.bn_stats(st[n][:, :], X[:, bass.ds(at(col(s, l, j)), D)]).then_inc(stats, 1)
            settle(dve, S["silu_a"])
            dve.wait_ge(stats, at(t + 1))
            dve.bn_aggr(mv[n][:, :], st[n][:, :]).then_inc(aggr, 1)

        def norm(s, l, j, n, sems):
            t = t_of(s, j)
            aggr, rstd, bc, scaled, normed, repeated = sems[1:]
            x, y, b = X[:, bass.ds(at(col(s, l, j)), D)], ys[n], (bF, mod2)[n]
            dve.wait_ge(aggr, at(t + 1))
            dve.wait_ge(bc, at(t + 1))
            dve.scalar_tensor_tensor(y[:, 0:D], x, mv[n][:, 0:1], b[:, 0, 0:D], ALU.subtract, ALU.mult).then_inc(scaled, 1)
            dve.wait_ge(scaled, at(t + 1))
            dve.wait_ge(rstd, at(t + 1))
            dve.scalar_tensor_tensor(y[:, 0:D], y[:, 0:D], rs[n][:, 0:1], b[:, 1, 0:D], ALU.mult, ALU.add).then_inc(normed, 1)
            dve.wait_ge(normed, at(t + 1))
            dve.tensor_copy(y[:, D:D + 2 * TAIL].rearrange("p (a n) -> p a n", a=2),
                            y[:, E0:D].unsqueeze(1).to_broadcast([P, 2, TAIL])).then_inc(repeated, 1)

        norm1 = [S[n] for n in "stats aggr rstd1 bc1 scaled normed spread".split()]
        norm2 = [S[n] for n in "stats2 aggr2 rstd2 mod2_out scaled2 normed2 spread2".split()]

        def moments_one(s, l, j):
            t = t_of(s, j)
            settle(dve, S["silu_a"])
            if not isinstance(t, Count):
                dve.wait_ge(S["x_in"], 16 if t < 4 else 64)
            previous(dve, S["resid2"], t - TILES + 1 if l else 0)
            moments(s, l, j, 0, norm1)

        def norm_one(s, l, j):
            previous(dve, S["y_turned"], t_of(s, j))
            norm(s, l, j, 0, norm1)

        def low(dst, turned, sem, hi_sem, n):
            dve.wait_ge(hi_sem, at(n))
            dve.tensor_tensor(dst[:, AL:BL + 1, :], turned[:, 0:2, :], dst[:, A:BB + 1, :].bitcast(F32), ALU.subtract)
            dve.tensor_tensor(dst[32:64, E, :], turned[32:64, 2, :], dst[32:64, E, :].bitcast(F32), ALU.subtract)\
                .then_inc(sem, 1)

        def turned(bank_):
            return bank_[:, 2, 0:3 * P].rearrange("p (k n) -> p k n", k=3)

        def head_norm(t, p):
            u = t - TILES
            z = bF[:, 0:2, 0:D].rearrange("p a (h d) -> p a h d", h=H)
            heads = lambda a: a[:, :].rearrange("p (a h) -> p a h", a=2).unsqueeze(3).to_broadcast([P, 2, H, HD])
            dve.wait_ge(S["qk_mm"], at(t + 1))
            dve.tensor_reduce(s1[:, :].rearrange("p (a h) -> p a h", a=2), z, AX.X, ALU.add).then_inc(S["qk_sum"], 1)
            dve.wait_ge(S["qk_sum"], at(u + 1))
            dve.tensor_scalar(mu[:, :], s1[:, :], 1.0 / HD, None, ALU.mult).then_inc(S["qk_mean"], 1)
            dve.wait_ge(S["qk_mean"], at(u + 1))
            for read in (S["qk_h"], S["qk_l"]):
                previous(dve, read, t - 1)
            for a in range(2):
                i = dve.tensor_tensor(qks2[p][:, a, :, :], z[:, a, :, :], heads(mu)[:, a, :, :], ALU.subtract)
            i.then_inc(S["qk_cent"], 1)

        def head_var(t, p):
            u = t - TILES
            dve.wait_ge(S["qk_sq"], at(u + 1))
            dve.tensor_reduce(s2[p][:, :].rearrange("p (a h) -> p a h", a=2), sq[:, :, :, :], AX.X, ALU.add).then_inc(S["qk_var"], 1)

        def head_norm_end(t, p):
            u = t - TILES
            heads = lambda a: a[:, :].rearrange("p (a h) -> p a h", a=2).unsqueeze(3).to_broadcast([P, 2, H, HD])
            dve.wait_ge(S["qk_rstd"], at(u + 1))
            for a in range(2):
                i = dve.tensor_tensor(qks2[p][:, a, :, :], qks2[p][:, a, :, :], heads(rq[p])[:, a, :, :], ALU.mult)
            i.then_inc(S["qk_unit"], 1)
            dve.wait_ge(S["qk_unit"], at(u + 1))
            dve.tensor_tensor(qks2[p][:, 0, :, :], qks2[p][:, 0, :, :], gg[:, :].unsqueeze(1).to_broadcast([P, H, HD]), ALU.mult)\
                .then_inc(S["qk_g"], 1)

        def split_v(t, p):
            dve.wait_ge(S["v_h"], at(t + 1))
            v = bF[:, 2, 0:D].rearrange("p (a n) -> p a n", a=HP)
            r = vr[:, :].rearrange("p (a n) -> p a n", a=HP)
            previous(dve, S["v_l"], t)
            dve.tensor_tensor(r, v, v1[p][:, :, 0:2 * HD], ALU.subtract).then_inc(S["v_r"], 1)

        def split_qk(t, l, p):
            dve.wait_ge(S["qk_h"], at(t + 1))
            if l == 0:
                q, k = (bF[:, a, 0:D].rearrange("p (h d) -> p h d", h=H) for a in range(2))
            else:
                q, k = qks2[p][:, 0, :, :], qks2[p][:, 1, :, :]
            dve.tensor_tensor(qks[:, 0, :, HD:2 * HD], q, qks[:, 0, :, 0:HD].bitcast(F32), ALU.subtract)
            dve.tensor_tensor(qks[:, 1, :, 2 * HD:3 * HD], k, qks[:, 1, :, 0:HD].bitcast(F32), ALU.subtract).then_inc(S["qk_l"], 1)

        def low_v(t, p):
            dve.wait_ge(S["v_m"], at(t + 1))
            dve.tensor_tensor(v3[p][:, :, :], vr[:, :].rearrange("p (a n) -> p a n", a=HP), v2[p][:, :, :], ALU.subtract)\
                .then_inc(S["v_l"], 1)

        def lay_q(t):
            dve.wait_ge(S["q_turned"], at(t + 1))
            previous(dve, S["scores1"], t)
            dve.tensor_copy(qT[64:128, :, :, 1, :], flat(bF)[64:128, :].rearrange("p (a b q) -> p a b q", a=HP, b=2))\
                .then_inc(S["q_lay2"], 1)

        def by_half(i):
            return (bB[:, i, :].rearrange("p (a n) -> p a n", n=N), halves(prob[:, :])[:, i, :].rearrange("p (a n) -> p a n", n=N),
                    halves(mx[:, :])[:, i, :])

        def row_max(t, i):
            z, _, m = by_half(i)
            dve.wait_ge(S[f"scores{i}"], at(t + 1))
            dve.tensor_reduce(m, z, AX.X, ALU.max).then_inc(S[f"maxed{i}"], 1)

        def shift(t, i):
            z, p, m = by_half(i)
            previous(dve, S[f"p_turned{i}"], t)
            dve.wait_ge(S[f"maxed{i}"], at(t + 1))
            dve.tensor_tensor(p, z, m.unsqueeze(2).to_broadcast([P, H // 2, N]), ALU.subtract).then_inc(S[f"shifted{i}"], 1)

        def low_p(t, i):
            dve.wait_ge(S[f"pT_h{i}"], at(t + 1))
            dve.tensor_tensor(pTl[:, 4 * i:4 * i + 4, :], bB[:, i, :].rearrange("p (a n) -> p a n", a=HP // 2),
                              pTh[:, 4 * i:4 * i + 4, :], ALU.subtract).then_inc(S[f"pT_l{i}"], 1)

        def low_y(t):
            low(yT, turned(bF), S["yTl"], S["yTh"], t + 1)

        def low_o(t):
            low(oT, turned(bB), S["oT_l"], S["oT_h"], t + 1)

        def low_y2(s, j):
            low(y2T[:, :, j * P:(j + 1) * P], turned(bB), S["y2T_l"], S["y2T_h"], t_of(s, j) + 1)

        def moments_two(s, l, j):
            settle(dve, S["silu_a"])
            dve.wait_ge(S["resid"], at(t_of(s, j) + 1))
            moments(s, l, j, 1, norm2)

        def norm_two(s, l, j):
            previous(dve, S["y2_turned"], t_of(s, j))
            norm(s, l, j, 1, norm2)

        def normalise(t):
            w = 2 * HD + 1
            dve.wait_ge(S["pv_mm"], at(t + 1))
            acc = (bB[:, 0:2, 0:HP * w // 2].rearrange("p i (a n) -> p i a n", n=w),
                   bB[:, 2, 0:HP * w].rearrange("p (i a n) -> p i a n", i=2, n=w))
            sums = rsum[:, :, :].rearrange("p b (i a) -> p b i a", i=2)
            for b in range(2):
                i = dve.reciprocal(sums[:, b, :, :], acc[b][:, :, :, 2 * HD])
            i.then_inc(S["recip"], 1)
            dve.wait_ge(S["recip"], at(t + 1))
            for h in range(2):
                src = slice(h * N, (h + 1) * N)
                for b in range(2):
                    dst = os_[b * N:(b + 1) * N, 0:D].rearrange("p (i a h d) -> p i a h d", i=2, h=2, d=HD)[:, :, :, h, :]
                    i = dve.tensor_tensor(dst, acc[b][src, :, :, h * HD:(h + 1) * HD],
                                          sums[src, b, :, :].unsqueeze(3).to_broadcast([N, 2, HP // 2, HD]), ALU.mult)
            i.then_inc(S["onormed"], 1)
            dve.wait_ge(S["onormed"], at(t + 1))
            dve.tensor_copy(os_[:, D:D + 2 * TAIL].rearrange("p (a n) -> p a n", a=2),
                            os_[:, E0:D].unsqueeze(1).to_broadcast([P, 2, TAIL])).then_inc(S["ospread"], 1)

        def add_attention(s, l, j):
            t = t_of(s, j)
            x = X[:, bass.ds(at(col(s, l, j)), D)]
            dve.wait_ge(S["proj_mm"], at(t + 1))
            dve.tensor_tensor(tmp[:, :], bB[:, 2, 0:D], gate1[:, :], ALU.mult).then_inc(S["gated"], 1)
            dve.wait_ge(S["gated"], at(t + 1))
            dve.tensor_tensor(x, x, tmp[:, :], ALU.add).then_inc(S["resid"], 1)

        def add_mlp(s, l, j):
            u = t_of(s, j) - 2
            x = X[:, bass.ds(at(col(s, l, j - 2)), D)]
            dve.wait_ge(S["gate2_out"], at(u + 1))
            dve.wait_ge(S["out_mm"], at(u + 1))
            previous(dve, S["resid2"], u)
            dve.tensor_tensor(tmp2[:, :], bM[:, j, 0:D], gate2[:, j, :], ALU.mult).then_inc(S["gated2"], 1)
            dve.wait_ge(S["gated2"], at(u + 1))
            dve.tensor_tensor(x, x, tmp2[:, :], ALU.add).then_inc(S["resid2"], 1)

        def slot_1a(s, back, layout, entry, mlp):
            t = t_of(s, 0)
            aside(s, 4)
            low_p(t, 0)
            lay_q(t + 1)
            low_p(t, 1)
            moments_one(s, entry, 2)
            normalise(t)
            norm_one(s, entry, 2)
            row_max(t + 1, 0)
            low_o(t)
            row_max(t + 1, 1)
            aside(s, 0)
            shift(t + 1, 0)
            low_y(t + 2)
            shift(t + 1, 1)
            add_attention(s, back, 0)
            moments_two(s, back, 0)
            norm_two(s, back, 0)
            aside(s, 1)
            split_v(t + 2, 0)
            if entry == 0:
                split_qk(t + 2, 0, 0)
            if entry == 1:
                head_norm(t + 2, 0)
            low_y2(s, 0)
            low_v(t + 2, 0)
            if entry == 1:
                head_var(t + 2, 0)

        def slot_1b(s, back, layout, entry, mlp):
            t = t_of(s, 0)
            low_p(t + 1, 0)
            lay_q(t + 2)
            low_p(t + 1, 1)
            moments_one(s, entry, 3)
            normalise(t + 1)
            norm_one(s, entry, 3)
            aside(s, 2)
            low_o(t + 1)
            row_max(t + 2, 0)
            low_y(t + 3)
            shift(t + 2, 0)
            add_attention(s, back, 1)
            row_max(t + 2, 1)
            moments_two(s, back, 1)
            shift(t + 2, 1)
            split_v(t + 3, 1)
            norm_two(s, back, 1)
            aside(s, 3)
            low_v(t + 3, 1)
            if mlp is not None:
                add_mlp(s, mlp, 0)
            low_y2(s, 1)
            split_qk(t + 3, 0, 1)
            if mlp is not None:
                add_mlp(s, mlp, 1)

        def slot_2a(s, back, layout, entry, mlp):
            t = t_of(s, 0)
            low_p(t, 0)
            if entry is not None:
                moments_one(s, entry, 2)
            low_p(t, 1)
            head_norm_end(t + 1, 1)
            if entry is not None:
                norm_one(s, entry, 2)
            normalise(t)
            if entry is not None:
                low_y(t + 2)
            split_qk(t + 1, 1, 1)
            low_o(t)
            if entry is not None:
                head_norm(t + 2, 0)
            add_attention(s, back, 0)
            aside(s, 6)
            if entry is not None:
                split_v(t + 2, 0)
            moments_two(s, back, 0)
            lay_q(t + 1)
            if entry is not None:
                head_var(t + 2, 0)
            norm_two(s, back, 0)
            row_max(t + 1, 0)
            shift(t + 1, 0)
            row_max(t + 1, 1)
            shift(t + 1, 1)
            low_y2(s, 0)
            if entry is not None:
                low_v(t + 2, 0)

        def slot_2b(s, back, layout, entry, mlp):
            t = t_of(s, 0)
            if entry is not None:
                moments_one(s, entry, 3)
            low_p(t + 1, 0)
            if layout[1] is not None:
                head_norm_end(t + 2, 0)
            low_p(t + 1, 1)
            if entry is not None:
                norm_one(s, entry, 3)
            normalise(t + 1)
            if entry is not None:
                low_y(t + 3)
            if layout[1] is not None:
                split_qk(t + 2, 1, 0)
            low_o(t + 1)
            if entry is not None:
                head_norm(t + 3, 1)
                split_v(t + 3, 1)
            add_attention(s, back, 1)
            if layout[1] is not None:
                lay_q(t + 2)
            moments_two(s, back, 1)
            if entry is not None:
                low_v(t + 3, 1)
            aside(s, 5)
            if entry is not None:
                head_var(t + 3, 1)
            norm_two(s, back, 1)
            if layout[1] is not None:
                row_max(t + 2, 0)
                shift(t + 2, 0)
                row_max(t + 2, 1)
                shift(t + 2, 1)
            low_y2(s, 1)
            add_mlp(s, mlp, 0)
            add_mlp(s, mlp, 1)

        def last(s):
            add_mlp(s, 1, 0)
            add_mlp(s, 1, 1)

        def wanted(l):
            cols = [(2 * D, (j - TILES * l) * D) for j in (-2, -1, 0, 1, 2, 3)]
            return [(2, -2), (2, -1), (2, 0), (2, 1), (2, 2), (2, 3), (2, 4)] + [(2, n - TILES) for n in (1, 2, 3, 4)] * l + cols

        def aside(s, place):
            if isinstance(s, Count) or s != (0, 0, 0, 0, PAIRS - 1, PAIRS, PAIRS + 1)[place]:
                return
            if place == 4:
                weights_qkv(1)
            elif place == 5:
                weights_w1(1)
            elif place == 6:
                weights_w2(1)
            elif place == 0:
                weights_w1(0)
            elif place == 1:
                weights_w2(0)
                low_bias(1)
            else:
                for m in range(3 * (place - 2), 3 * (place - 1)):
                    modulation(1, m)

        def before(s):
            if s == PAIRS:
                weights_out(1)

        dve.memset(half[:, :], -0.5)
        dve.memset(onesf[:, :], 1.0)
        dve.memset(plus[:, :], 1.0)
        dve.memset(mask[0:32, :], 0.0)
        dve.memset(mask[32:64, 0:1], -1.0)
        dve.memset(mask[32:64, 1:2], 0.0)
        dve.memset(mask[64:96, :], -1.0)
        dve.memset(ones[:, :].bitcast(F32), 1.0)
        for t_ in (ys[0], ys[1], os_):
            dve.memset(t_[:, D + 2 * TAIL:3 * P], 1.0)
        for v in v1:
            i = dve.memset(v[:, :, 2 * HD:2 * HD + 1], 1.0)
        i.then_inc(S["consts"], 1)
        dve.memset(qks[:, :, :, 3 * HD:SLOT].bitcast(F32), 0.0)
        dve.memset(qT[0:64, :, :, 1, :].bitcast(F32), 0.0)
        dve.memset(qT[64:128, :, :, 0, :].bitcast(F32), 0.0).then_inc(S["pads"], 1)
        dve.wait_ge(S["silu_a"], 1)
        dve.tensor_scalar(c1[:, :], c1[:, :], 1.0, None, ALU.add).then_inc(S["silu_b"], 1)
        dve.wait_ge(S["silu_b"], 1)
        dve.reciprocal(c1[:, :], c1[:, :]).then_inc(S["silu_c"], 1)
        dve.wait_ge(S["silu_c"], 1)
        dve.tensor_tensor(c0[:, :], c0[:, :], c1[:, :], ALU.mult).then_inc(S["silu_d"], 1)
        dve.wait_ge(S["c_turned"], 1)
        for k in range(3):
            i = dve.tensor_copy(cT[:, k, :].rearrange("p (r n) -> p r n", r=3),
                                bB[0:96, 2, k * 32:(k + 1) * 32].unsqueeze(1).to_broadcast([96, 3, 32]))
        i.then_inc(S["c_copied"], 1)
        low_bias(0)
        modulation(0, 0)
        modulation(0, 1)
        moments_one(0, 0, 0)
        norm_one(0, 0, 0)
        modulation(0, 2)
        weights_qkv(0)
        low_y(0)
        modulation(0, 3)
        weights_out(0)
        split_v(0, 0)
        split_qk(0, 0, 0)
        low_v(0, 0)
        modulation(0, 4)
        lay_q(0)
        moments_one(0, 0, 1)
        norm_one(0, 0, 1)
        modulation(0, 5)
        low_y(1)
        for i in range(2):
            row_max(0, i)
        for i in range(2):
            shift(0, i)
        split_v(1, 1)
        split_qk(1, 0, 1)
        low_v(1, 1)
        steps(dve, (slot_1a, slot_1b, slot_2a, slot_2b), last, wanted, before)


_OUT = ((B, N, D), "float32")


def kernel(**inputs):
    import numpy as _np
    import concourse.bacc as _bacc
    from concourse import mybir as _mybir
    from concourse.bass_utils import run_bass_kernel_spmd as _run

    nc = _bacc.Bacc("TRN2", target_bir_lowering=False, num_devices=1)
    arrays, io = {}, {}
    for name, value in inputs.items():
        a = _np.ascontiguousarray(value)
        arrays[f"in_{name}_dram"] = a
        io[name] = nc.dram_tensor(f"in_{name}_dram", a.shape, _mybir.dt.from_np(a.dtype), kind="ExternalInput").ap()
    shape, dtype = _OUT
    out = nc.dram_tensor("out_0_dram", shape, _mybir.dt.from_np(_np.dtype(dtype)), kind="ExternalOutput").ap()
    build(nc, io, out)
    r = _run(nc, [arrays], core_ids=[0])
    return r.results[0]["out_0_dram"]
```
